# Optimizing a Trainium2 kernel written in Bass

```python
import numpy as np
import jax
import jax.numpy as jnp

def _softmax(x, axis=-1):
    return jax.nn.softmax(x, axis=axis)

def _gelu(x):
    return jax.nn.gelu(x, approximate=True)

def _silu(x):
    return jax.nn.silu(x)

def _sigmoid(x):
    return jax.nn.sigmoid(x)

def _layernorm(x, axis=-1, eps=1e-05):
    m = jnp.mean(x, axis=axis, keepdims=True)
    v = jnp.var(x, axis=axis, keepdims=True)
    return (x - m) / jnp.sqrt(v + eps)

def _scatter_add(tgt, idx, src, axis=0):
    return tgt.at[idx].add(src)

def _segment_sum(src, seg, n):
    return jax.ops.segment_sum(src, seg, n)
kernel_name = 'mk_adaln_ffn_d1_seqx_r4_291817'

def setup_inputs(seed: int=0):
    np.random.seed(seed)
    _w = jnp.asarray

    def _rec_inputs():
        import jax
        import jax.numpy as jnp
        _rk = jax.random.key(seed)
        x = 7.22e-05 + 1 * jax.random.normal(jax.random.fold_in(_rk, 1), (2, 1024, 256), jnp.float32)
        _lenS = 1024 - jax.random.randint(jax.random.fold_in(_rk, 7), (2,), 0, max(1, 1024 // 4) + 1, jnp.int32)
        _lenS2 = 1024 - jax.random.randint(jax.random.fold_in(_rk, 8), (2,), 0, max(1, 1024 // 4) + 1, jnp.int32)
        cond_8 = jax.random.uniform(jax.random.fold_in(_rk, 11), (2, 8), jnp.float32, 0.0, 0.999837)
        return (x, cond_8)
    x, cond_8 = _rec_inputs()

    def _L0_cond_setup():
        import jax, jax.numpy as jnp
        import numpy as np
        key = jax.random.key(seed)
        k1, k2, k3, k4, k5 = jax.random.split(key, 5)
        B, N, T, O, G = (32, 64, 256, 256, 8)
        x = jax.random.normal(k1, (B, N, T), dtype=jnp.float32)
        y = jax.random.uniform(k2, (B, G), dtype=jnp.float32)
        weight = jax.random.normal(k3, (G, O, T), dtype=jnp.float32) * (1.0 / np.sqrt(T))
        mask = jax.random.uniform(k4, (O, T), dtype=jnp.float32)
        bias = jax.random.normal(k5, (O,), dtype=jnp.float32)
        return {'x': x, 'y': y, 'weight': weight, 'mask': mask, 'bias': bias}
    _L0_cond_all = _L0_cond_setup()
    _L0_cond_in = {k: v for k, v in _L0_cond_all.items() if k in ('weight', 'mask', 'bias')}
    del _L0_cond_all

    def _L0_ffn_setup():
        import jax, jax.numpy as jnp
        import numpy as np
        B, S, D, H, E = (4, 512, 256, 1024, 8)
        key = jax.random.key(seed)
        ks = jax.random.split(key, 8)
        s_d = 1.0 / np.sqrt(D)
        s_h = 1.0 / np.sqrt(H)
        return {'x': jax.random.normal(ks[0], (B, S, D), dtype=jnp.float32), 'gate_w': jax.random.uniform(ks[1], (E, D), jnp.float32, -s_d, s_d), 'gate_b': jax.random.uniform(ks[2], (E,), jnp.float32, -s_d, s_d), 'w1': jax.random.uniform(ks[3], (E, H, D), jnp.float32, -s_d, s_d), 'b1': jax.random.uniform(ks[4], (E, H), jnp.float32, -s_d, s_d), 'w2': jax.random.uniform(ks[5], (E, D, H), jnp.float32, -s_h, s_h), 'b2': jax.random.uniform(ks[6], (E, D), jnp.float32, -s_h, s_h)}
    _L0_ffn_all = _L0_ffn_setup()
    _L0_ffn_in = {k: v for k, v in _L0_ffn_all.items() if k in ('gate_w', 'gate_b', 'w1', 'b1', 'w2', 'b2')}
    del _L0_ffn_all
    return {'x': x, 'cond_8': cond_8, 'L0_cond_weight': _L0_cond_in['weight'], 'L0_cond_mask': _L0_cond_in['mask'], 'L0_cond_bias': _L0_cond_in['bias'], 'L0_ffn_gate_w': _L0_ffn_in['gate_w'], 'L0_ffn_gate_b': _L0_ffn_in['gate_b'], 'L0_ffn_w1': _L0_ffn_in['w1'], 'L0_ffn_b1': _L0_ffn_in['b1'], 'L0_ffn_w2': _L0_ffn_in['w2'], 'L0_ffn_b2': _L0_ffn_in['b2']}

def reference(x, cond_8, L0_cond_weight, L0_cond_mask, L0_cond_bias, L0_ffn_gate_w, L0_ffn_gate_b, L0_ffn_w1, L0_ffn_b1, L0_ffn_w2, L0_ffn_b2):
    import jax
    import jax.numpy as jnp

    def _L0_cond_ref(x, y, weight, mask, bias):
        import jax, jax.numpy as jnp
        import numpy as np
        masked_w = weight * mask[None, :, :]
        w_bot = jnp.einsum('bg,got->bot', y, masked_w)
        return jnp.einsum('bnt,bot->bno', x, w_bot) + bias

    def _L0_ffn_ref(x, gate_w, gate_b, w1, b1, w2, b2):
        import jax, jax.numpy as jnp
        import numpy as np
        B, S, D, H, E = (4, 512, 256, 1024, 8)
        b, s, d = x.shape
        xf = x.reshape(-1, d)
        logits = xf @ gate_w.T + gate_b
        top1 = jnp.argmax(logits, axis=-1)
        out = jnp.zeros_like(xf)
        n_experts = w1.shape[0]
        for e in range(n_experts):
            h = jax.nn.relu(xf @ w1[e].T + b1[e])
            y = h @ w2[e].T + b2[e]
            out = out + jnp.where((top1 == e)[:, None], y, jnp.zeros((), y.dtype))
        return out.reshape(b, s, d)
    x = x + _L0_ffn_ref(_L0_cond_ref(x, cond_8, L0_cond_weight, L0_cond_mask, L0_cond_bias), L0_ffn_gate_w, L0_ffn_gate_b, L0_ffn_w1, L0_ffn_b1, L0_ffn_w2, L0_ffn_b2)
    return x

_drawn_inputs = setup_inputs


def setup_inputs(seed=0):
    import zlib

    import numpy as np

    out = dict(_drawn_inputs(seed))
    spreads = {}
    factors = {'L0_ffn_b1': 4.216, 'L0_ffn_b2': 3.278}
    for name, (base, spread) in spreads.items():
        noise = np.random.default_rng([zlib.crc32(name.encode()), seed]).standard_normal(out[name].shape)
        drawn = base * np.exp(spread * noise) if base else spread * noise
        out[name] = jnp.asarray(drawn.astype(out[name].dtype))
    for name, factor in factors.items():
        out[name] = (out[name] * factor).astype(out[name].dtype)
    return out
```

```python
from contextlib import ExitStack

import concourse.bass as bass
from concourse import mybir

ALU = mybir.AluOpType
ACT = mybir.ActivationFunctionType
AX = mybir.AxisListType
F32 = mybir.dt.float32
F16 = mybir.dt.float16
BF16 = mybir.dt.bfloat16
I32 = mybir.dt.int32

P = 128
B, S, D = 2, 1024, 256
E, H, G = 8, 1024, 8
TOK = B * S
TT = TOK // P
TPB = S // P
KD = D // P
KH = H // P
SLOT_TILES = TOK // P + E - 1
ST = SLOT_TILES + 1
RW = D + E
WE = 2 * D * H // P
W1E = D * H // P
CW = KD * D
WSCALE = 64.0
RAW_RING = 2


def build(nc, x_t, x_rows, cond_y, cond_w, cond_mask, cond_bias, gate_t, gate_b, w_all, b1_t, b2, out):
    xf_rows = nc.dram_tensor("xf_rows", [TOK, D], F32, kind="Internal").ap()
    with ExitStack() as ctx:
        def sb(name, shape, dt=F32):
            return ctx.enter_context(nc.sbuf_tensor(name, shape, dt))

        def sem(name):
            return ctx.enter_context(nc.semaphore(name))

        wsplit = sb("wsplit", [P, E, 2, WE], F16)
        shared = sb("shared", [P, RAW_RING * WE])
        rows = sb("rows", [P, TT * RW])
        early = sb("early", [P, 2 * CW + 2 * KD * RW + CW])
        xT = wsplit[:, E - 2, :, :].rearrange("p a n -> p (a n)").bitcast(F32).rearrange("p (k n) -> p k n", k=KD)
        condw = wsplit[:, E - 1, :, :].rearrange("p a n -> p (a n)").bitcast(F32).rearrange("p (g n) -> p g n", g=G)
        raw = shared[:, :].rearrange("p (r n) -> p r n", r=RAW_RING)
        w1s = shared[:, 0:2 * W1E].bitcast(F16).rearrange("p (b a n) -> p b a n", b=2, a=2)
        act_f = shared[:, 2 * W1E:2 * W1E + KH * P]
        hT = shared[:, 2 * W1E + KH * P:2 * W1E + 3 * KH * P].bitcast(F16).rearrange(
            "p (b a n) -> p b a n", b=2, a=2)
        xfl = rows[:, :].rearrange("p (t n) -> p t n", n=RW)
        diag = rows[:, 0:G * P].rearrange("p (g n) -> p g n", g=G)
        b2_all = rows[:, 0:E * D].rearrange("p (e n) -> p e n", e=E)
        wbot = early[:, 0:2 * CW].rearrange("p (b k n) -> p b k n", b=B, k=KD)
        rhs = early[:, 2 * CW:2 * CW + 2 * KD * RW].rearrange("p (b k n) -> p b k n", b=B, k=KD)
        mask = early[:, 2 * CW + 2 * KD * RW:]
        oh_slot = early[:, 0:TT * P // 2].bitcast(BF16).rearrange("p (t n) -> p t n", t=TT)

        y_all = sb("y_all", [P, B * G])
        gate = sb("gate", [P, KD, E])
        bias_col = sb("bias_col", [P, KD])
        bias_mat = sb("bias_mat", [P, KD, P])
        row_bias = sb("row_bias", [P, RW])
        gate_bias = sb("gate_bias", [P, E])
        b1_raw = sb("b1_raw", [P, E, KH])
        b1_s = sb("b1_s", [P, E, KH])
        ident = sb("ident", [P, P])
        ones = sb("ones", [P, P])
        before = sb("before", [P, P], BF16)
        ones_h = sb("ones_h", [P, P], BF16)
        iota_r = sb("iota_r", [P, P], BF16)
        e_less_8 = sb("e_less_8", [P, E])
        tile_no = sb("tile_no", [P, ST])
        tile_at = sb("tile_at", [P, ST])
        tok_tile = sb("tok_tile", [P, TT])
        part_no = sb("part_no", [P, 1])

        best = sb("best", [P, TT])
        pick = sb("pick", [P, TT, E])
        first = sb("first", [P, TT])
        oh = sb("oh", [P, E, TT], BF16)
        count = sb("count", [P, E])
        per_tile = sb("per_tile", [P, E * TT])
        upto = sb("upto", [P, E, TT])
        padded_i = sb("padded_i", [P, 2, E], I32)
        padded = sb("padded", [P, E])
        ends = sb("ends", [P, E])
        offs = sb("offs", [P, 3, E])
        place = sb("place", [P, E, TT])
        slot_f = sb("slot_f", [P, TT])
        slot_i = sb("slot_i", [P, 3, TT], I32)
        slot_lo = sb("slot_lo", [P, TT])
        slot_hi = sb("slot_hi", [P, TT])
        sel = sb("sel", [P, TT, ST])
        tok_rhs = sb("tok_rhs", [P, TT, 2 * ST], BF16)
        tok_f = sb("tok_f", [P, 2 * ST])
        tok_sum = sb("tok_sum", [P, ST])
        tok_of_slot = sb("tok_of_slot", [P, ST], I32)
        past = sb("past", [P, ST, E])
        tile_e = sb("tile_e", [P, ST])
        tile_expert = sb("tile_expert", [P, ST], I32)

        xg = sb("xg", [P, 2, D])
        res = sb("res", [P, 2, D])
        xs = sb("xs", [P, 2, 2, D], F16)

        psum = ctx.enter_context(nc.psum_tensor("psum", [P, 8, 512], F32))
        ps_cond, ps_prefix, ps_xT = psum[:, 0, :], psum[:, 0, 0:E * TT], psum[:, 0, 0:D]
        ps_wT = [psum[:, 1, :], psum[:, 2, :]]
        ps_count, ps_tok = psum[:, 1, 0:E * TT], psum[:, 2, 0:2 * ST]
        ps_gate = psum[:, 3, 0:2 * KD * E + E]
        ps_rows = [psum[:, 4 + n, 0:RW] for n in range(4)]
        ps_h = [[psum[:, 1 + 2 * n + q, :] for q in range(2)] for n in range(2)]
        ps_y = [psum[:, 5 + n, 0:D] for n in range(2)]

        ld_y, ld_mask, ld_small, ld_b1, ld_b2 = map(sem, ["ld_y", "ld_mask", "ld_small", "ld_b1", "ld_b2"])
        ld_cw = [sem(f"ld_cw{n}") for n in range(4)]
        ld_x = [sem(f"ld_x{n}") for n in range(B)]
        ld_raw = [sem(f"ld_raw{e}") for e in range(E)]
        consts = sem("consts")
        pool_step = sem("pool_step")
        diag_ready = sem("diag_ready")
        cond_acc = sem("cond_acc")
        cond_ps = sem("cond_ps")
        wbot_ready = sem("wbot_ready")
        wT_ps = sem("wT_ps")
        wT_ready = sem("wT_ready")
        bias_ready = sem("bias_ready")
        gate_ps = sem("gate_ps")
        rhs_ready = sem("rhs_ready")
        rows_ps = sem("rows_ps")
        rows_ready = sem("rows_ready")
        rows_stored = sem("rows_stored")
        hi_ready = sem("hi_ready")
        split_ready = sem("split_ready")
        oh_ready = sem("oh_ready")
        rank_ps = sem("rank_ps")
        dve_step = sem("dve_step")
        tok_rhs_ready = sem("tok_rhs_ready")
        tok_ps = sem("tok_ps")
        routed = sem("routed")
        x_in = [sem(f"x_in{n}") for n in range(2)]
        res_in = [sem(f"res_in{n}") for n in range(2)]
        res_ready = sem("res_ready")
        xT_ps = sem("xT_ps")
        xhi_ready = sem("xhi_ready")
        xlo_ready = sem("xlo_ready")
        w1_ready = sem("w1_ready")
        h_ps = sem("h_ps")
        h_sum = sem("h_sum")
        hhi_ready = sem("hhi_ready")
        hlo_ready = sem("hlo_ready")
        y_ps = sem("y_ps")
        y_ready = sem("y_ready")
        stored = [sem(f"stored{n}") for n in range(2)]

        N_CONST = 9
        block = ctx.enter_context(nc.Block())

        @block.sync
        def _(sp):
            sp.dma_start(y_all[:, :], cond_y.partition_broadcast(P)).then_inc(ld_y, 16)
            for n in range(4):
                sp.dma_start(condw[:, 2 * n:2 * n + 2, :], cond_w[n]).then_inc(ld_cw[n], 16)
                if n == 0:
                    sp.dma_start(mask, cond_mask).then_inc(ld_mask, 16)
            for b in range(B):
                sp.dma_start(xT[:, :, b * S:(b + 1) * S], x_t[:, :, b * S:(b + 1) * S]).then_inc(ld_x[b], 16)
            for e in range(E):
                if e >= RAW_RING:
                    sp.wait_ge(split_ready, e - RAW_RING + 1)
                sp.dma_start(raw[:, e % RAW_RING, :], w_all[e]).then_inc(ld_raw[e], 16)
            sp.wait_ge(routed, 1)
            sp.wait_ge(rows_stored, 64)
            sp.dma_start(b2_all, b2.partition_broadcast(P)).then_inc(ld_b2, 16)

        @block.gpsimd
        def _(pool):
            g = nc.gpsimd
            g.memset(ident[:, :], 0.0).then_inc(pool_step, 1)
            g.memset(ones[:, :], 1.0).then_inc(consts, 1)
            g.memset(ones_h[:, :], 1.0).then_inc(pool_step, 1)
            pool.wait_ge(pool_step, 2)
            g.affine_select(out=ident[:, :], in_=ident[:, :], compare_op=ALU.not_equal, fill=1.0, base=0,
                            pattern=[[-1, P]], channel_multiplier=1).then_inc(consts, 1)
            g.affine_select(out=before[:, :], in_=ones_h[:, :], compare_op=ALU.is_gt, fill=0.0, base=0,
                            pattern=[[1, P]], channel_multiplier=-1).then_inc(consts, 1)

            def iota(t, pattern, base=0, cm=0):
                g.iota(t, pattern, base=base, channel_multiplier=cm,
                       allow_small_or_imprecise_dtypes=True).then_inc(consts, 1)

            iota(iota_r[:, :], [[1, P]])
            iota(e_less_8[:, :], [[1, E]], base=-E)
            iota(tile_no[:, :], [[1, ST]])
            iota(tile_at[:, :], [[P, ST]])
            iota(tok_tile[:, :], [[1, TT]], base=-TT)
            iota(part_no[:, :], [[0, 1]], cm=1)
            g.memset(xg[:, :, :], 0.0).then_inc(pool_step, 1)
            g.memset(res[:, :, :], 0.0).then_inc(pool_step, 1)
            for n in range(4):
                pool.wait_ge(rows_ready, 4 * n + 4)
                pool.dma_start(xf_rows[4 * n * P:(4 * n + 4) * P, :].rearrange("(t p) d -> p t d", p=P),
                               xfl[:, 4 * n:4 * n + 4, 0:D]).then_inc(rows_stored, 16)

            def gather_x(i):
                if i >= 2:
                    pool.wait_ge(xT_ps, i - 1)
                g.indirect_dma_start(xg[:, i % 2, :], None, xf_rows,
                                     bass.IndirectOffsetOnAxis(ap=tok_of_slot[:, i:i + 1], axis=0),
                                     bounds_check=TOK - 1, oob_is_err=False).then_inc(x_in[i % 2], 16)

            def gather_res(i):
                if i >= 2:
                    pool.wait_ge(stored[i % 2], 16 * (i // 2))
                g.indirect_dma_start(res[:, i % 2, :], None, x_rows,
                                     bass.IndirectOffsetOnAxis(ap=tok_of_slot[:, i:i + 1], axis=0),
                                     bounds_check=TOK - 1, oob_is_err=False).then_inc(res_in[i % 2], 16)

            def add_b2(i):
                e = pool.value_load(tile_expert[0:1, i:i + 1], min_val=0, max_val=E - 1)
                pool.wait_ge(res_in[i % 2], 16 * (i // 2 + 1))
                g.tensor_tensor(res[:, i % 2, :], res[:, i % 2, :],
                                b2_all[:, bass.ds(e, 1), :].rearrange("p a n -> p (a n)"), ALU.add).then_inc(res_ready, 1)

            def scatter(i):
                pool.wait_ge(y_ready, i + 1)
                g.indirect_dma_start(out, bass.IndirectOffsetOnAxis(ap=tok_of_slot[:, i:i + 1], axis=0),
                                     res[:, i % 2, :], None,
                                     bounds_check=TOK - 1, oob_is_err=False).then_inc(stored[i % 2], 16)

            pool.wait_ge(pool_step, 4)
            pool.wait_ge(rows_stored, 64)
            pool.wait_ge(routed, 1)
            gather_x(0)
            gather_x(1)
            gather_res(0)
            pool.wait_ge(ld_b2, 16)
            add_b2(0)
            for i in range(SLOT_TILES):
                if i + 2 < SLOT_TILES:
                    gather_x(i + 2)
                if i + 1 < SLOT_TILES:
                    gather_res(i + 1)
                    add_b2(i + 1)
                scatter(i)
            for n in range(2):
                pool.wait_ge(stored[n], 16 * ((SLOT_TILES - n + 1) // 2))

        @block.scalar
        def _(act):
            a = nc.scalar
            act.dma_start(gate[:, :, :], gate_t).then_inc(ld_small, 16)
            act.dma_start(bias_col[:, :], cond_bias.rearrange("(k p) -> p k", p=P),
                          allow_slow_non_contiguous=True).then_inc(ld_small, 16)
            act.dma_start(row_bias[:, 0:D], cond_bias.partition_broadcast(P)).then_inc(ld_small, 16)
            act.dma_start(gate_bias[:, :], gate_b.partition_broadcast(P)).then_inc(ld_small, 16)
            act.dma_start(b1_raw[:, :, :], b1_t).then_inc(ld_b1, 16)
            act.wait_ge(consts, 2)
            act.wait_ge(ld_y, 16)
            for n in range(G):
                a.mul(diag[:, n, :], ident[:, :], y_all[:, G + n:G + n + 1]).then_inc(diag_ready, 1)
            act.wait_ge(ld_b1, 16)
            a.mul(b1_s[:, :, :], b1_raw[:, :, :], WSCALE).then_inc(bias_ready, 1)
            for b in range(B):
                act.wait_ge(wT_ps, b + 1)
                a.copy(rhs[:, b, :, 0:D], ps_wT[b].rearrange("p (k n) -> p k n", k=KD)).then_inc(wT_ready, 1)

            def weights_hi(e):
                act.wait_ge(ld_raw[e], 16)
                for q in range(4):
                    n = WE // 4
                    last = a.mul(wsplit[:, e, 0, q * n:(q + 1) * n], raw[:, e % RAW_RING, q * n:(q + 1) * n], WSCALE)
                last.then_inc(hi_ready, 1)

            for e in range(E):
                if e == E - 2:
                    act.wait_ge(rows_ps, TT)
                weights_hi(e)

            def x_hi(i, b):
                act.wait_ge(xT_ps, i + 1)
                if not isinstance(i, int) or i >= 2:
                    act.wait_ge(h_ps, 2 * i - 2)
                a.copy(xs[:, b, 0, :], ps_xT).then_inc(xhi_ready, 1)

            def h_hi(i, b):
                if not isinstance(i, int) or i >= 2:
                    act.wait_ge(y_ps, i - 1)
                for q in range(2):
                    act.wait_ge(h_sum, 2 * i + q + 1)
                    a.activation(hT[:, b, 0, q * 512:(q + 1) * 512], act_f[:, q * 512:(q + 1) * 512],
                                 ACT.Relu).then_inc(hhi_ready, 1)

            x_hi(0, 0)
            x_hi(1, 1)
            h_hi(0, 0)

            def tile(i, b):
                x_hi(i + 1, 1 - b)
                h_hi(i, b)

            tile(1, 1)
            with act.Fori(1, (SLOT_TILES - 1) // 2) as j:
                tile(2 * j, 0)
                tile(2 * j + 1, 1)
            h_hi(SLOT_TILES - 1, (SLOT_TILES - 1) % 2)

        @block.vector
        def _(dve):
            v = nc.vector
            step = [0]

            def then(ins):
                ins.then_inc(dve_step, 1)
                step[0] += 1
                dve.wait_ge(dve_step, step[0])

            dve.wait_ge(ld_y, 16)
            acc = wbot[:, 0, :, :].rearrange("p k n -> p (k n)")
            for n in range(G):
                if n % 2 == 0:
                    dve.wait_ge(ld_cw[n // 2], 16)
                if n == 0:
                    then(v.tensor_scalar(acc, condw[:, 0, :], y_all[:, 0:1], None, ALU.mult))
                else:
                    then(v.scalar_tensor_tensor(acc, condw[:, n, :], y_all[:, n:n + 1], acc, ALU.mult, ALU.add))
            dve.wait_ge(ld_mask, 16)
            v.tensor_tensor(acc, acc, mask, ALU.mult).then_inc(wbot_ready, 1)
            dve.wait_ge(cond_ps, 1)
            v.tensor_tensor(wbot[:, 1, :, :].rearrange("p k n -> p (k n)"), ps_cond, mask, ALU.mult).then_inc(wbot_ready, 1)
            dve.wait_ge(ld_small, 64)
            dve.wait_ge(consts, 1)
            for k in range(KD):
                last = v.tensor_scalar(bias_mat[:, k, :], ones[:, :], bias_col[:, k:k + 1], None, ALU.mult)
            last.then_inc(bias_ready, 1)
            dve.wait_ge(gate_ps, 1)
            v.tensor_copy(rhs[:, :, :, D:RW], ps_gate[:, 0:2 * KD * E].rearrange("p (b k e) -> p b k e", b=B, k=KD)).then_inc(rhs_ready, 1)
            then(v.tensor_tensor(row_bias[:, D:RW], ps_gate[:, 2 * KD * E:], gate_bias[:, :], ALU.add))

            def weights_lo(e):
                dve.wait_ge(hi_ready, e + 1)
                for q in range(4):
                    n = WE // 4
                    last = v.scalar_tensor_tensor(wsplit[:, e, 1, q * n:(q + 1) * n],
                                                  raw[:, e % RAW_RING, q * n:(q + 1) * n], WSCALE,
                                                  wsplit[:, e, 0, q * n:(q + 1) * n], ALU.mult, ALU.subtract)
                last.then_inc(split_ready, 1)

            for t in range(TT):
                dve.wait_ge(rows_ps, t + 1)
                v.tensor_tensor(xfl[:, t, :], ps_rows[t % 4], row_bias[:, :], ALU.add).then_inc(rows_ready, 1)
                if t == 7:
                    weights_lo(0)

            logits = xfl[:, :, D:RW]

            def over_e(t):
                return t.unsqueeze(2).to_broadcast([P, TT, E])

            e_bc = e_less_8[:, :].unsqueeze(1).to_broadcast([P, TT, E])
            dve.wait_ge(rows_ready, TT)
            dve.wait_ge(consts, N_CONST)
            then(v.tensor_reduce(best[:, :], logits, AX.X, ALU.max))
            then(v.tensor_tensor(pick[:, :, :], logits, over_e(best[:, :]), ALU.is_equal))
            then(v.tensor_tensor(pick[:, :, :], pick[:, :, :], e_bc, ALU.mult))
            then(v.tensor_reduce(first[:, :], pick[:, :, :], AX.X, ALU.min))
            v.tensor_tensor(oh[:, :, :].rearrange("p e t -> p t e"), e_bc, over_e(first[:, :]),
                            ALU.is_equal).then_inc(oh_ready, 1)

            dve.wait_ge(rank_ps, 1)
            then(v.tensor_copy(per_tile[:, :], ps_count))
            v.tensor_reduce(count[:, :], per_tile[:, :].rearrange("p (e t) -> p e t", e=E), AX.X, ALU.add)
            upto_f = upto[:, :, :].rearrange("p e t -> p (e t)")
            then(v.tensor_tensor_scan(upto_f, ones[:, 0:E * TT], per_tile[:, :], 0.0, ALU.mult, ALU.add))
            then(v.tensor_scalar(padded_i[:, 0, :], count[:, :], float(P - 1), None, ALU.add))
            then(v.tensor_scalar(padded_i[:, 1, :], padded_i[:, 0, :], -P, None, ALU.bitwise_and))
            then(v.tensor_copy(padded[:, :], padded_i[:, 1, :]))
            v.tensor_tensor(offs[:, 1, :], upto[:, :, TT - 1], count[:, :], ALU.subtract)
            then(v.tensor_tensor_scan(ends[:, :], ones[:, 0:E], padded[:, :], 0.0, ALU.mult, ALU.add))
            then(v.tensor_tensor(offs[:, 0, :], ends[:, :], padded[:, :], ALU.subtract))
            then(v.tensor_tensor(offs[:, 2, :], offs[:, 0, :], offs[:, 1, :], ALU.subtract))
            place_f = place[:, :, :].rearrange("p e t -> p (e t)")
            then(v.tensor_tensor(place_f, upto_f, per_tile[:, :], ALU.subtract))
            then(v.tensor_tensor(place_f, ps_prefix, place_f, ALU.add))
            then(v.tensor_tensor(place[:, :, :], place[:, :, :], offs[:, 2, :].unsqueeze(2).to_broadcast([P, E, TT]), ALU.add))
            then(v.tensor_tensor(place[:, :, :], place[:, :, :], oh[:, :, :], ALU.mult))
            then(v.tensor_reduce(slot_f[:, :], place[:, :, :].rearrange("p e t -> p t e"), AX.X, ALU.add))
            then(v.tensor_copy(slot_i[:, 0, :], slot_f[:, :]))
            v.tensor_scalar(slot_i[:, 1, :], slot_i[:, 0, :], P - 1, None, ALU.bitwise_and)
            then(v.tensor_scalar(slot_i[:, 2, :], slot_i[:, 0, :], 7, None, ALU.logical_shift_right))
            v.tensor_copy(slot_lo[:, :], slot_i[:, 1, :])
            then(v.tensor_copy(slot_hi[:, :], slot_i[:, 2, :]))
            then(v.tensor_tensor(sel[:, :, :], tile_no[:, :].unsqueeze(1).to_broadcast([P, TT, ST]),
                                 slot_hi[:, :].unsqueeze(2).to_broadcast([P, TT, ST]), ALU.is_equal))
            v.tensor_scalar(tok_rhs[:, :, 0:ST], sel[:, :, :], part_no[:, 0:1], None, ALU.mult)
            v.tensor_tensor(tok_rhs[:, :, ST:2 * ST], sel[:, :, :],
                            tok_tile[:, :].unsqueeze(2).to_broadcast([P, TT, ST]), ALU.mult).then_inc(tok_rhs_ready, 1)
            for t in range(TT):
                v.tensor_scalar(oh_slot[:, t, :], iota_r[:, :], slot_lo[:, t:t + 1], None, ALU.is_equal).then_inc(tok_rhs_ready, 1)
            then(v.tensor_tensor(past[:, :, :], ends[:, :].unsqueeze(1).to_broadcast([P, ST, E]),
                                 tile_at[:, :].unsqueeze(2).to_broadcast([P, ST, E]), ALU.is_le))
            then(v.tensor_reduce(tile_e[:, :], past[:, :, :], AX.X, ALU.add))
            v.tensor_scalar(tile_expert[:, :], tile_e[:, :], float(E - 1), None, ALU.min)
            dve.wait_ge(tok_ps, 1)
            then(v.tensor_copy(tok_f[:, :], ps_tok))
            then(v.scalar_tensor_tensor(tok_sum[:, :], tok_f[:, ST:2 * ST], float(P), tok_f[:, 0:ST], ALU.mult, ALU.add))
            v.tensor_scalar(tok_of_slot[:, :], tok_sum[:, :], float(TOK), None, ALU.add).then_inc(routed, 1)
            for e in range(1, E):
                weights_lo(e)

            dve.wait_ge(split_ready, E)
            dve.wait_ge(routed, 1)
            dve.wait_ge(bias_ready, 2)

            def expert(i):
                return dve.value_load(tile_expert[0:1, bass.ds(i, 1)], min_val=0, max_val=E - 1)

            def w1_copy(i, b):
                e = expert(i)
                if not isinstance(i, int) or i >= 2:
                    dve.wait_ge(h_ps, 2 * i - 2)
                v.tensor_copy(w1s[:, b, :, :], wsplit[:, bass.ds(e, 1), :, 0:W1E].rearrange("p o a n -> p (o a) n")).then_inc(w1_ready, 1)

            def x_lo(i, b):
                dve.wait_ge(xhi_ready, i + 1)
                v.tensor_tensor(xs[:, b, 1, :], ps_xT, xs[:, b, 0, :], ALU.subtract).then_inc(xlo_ready, 1)

            def add_b1(i, b):
                e = expert(i)
                for q in range(2):
                    dve.wait_ge(h_ps, 2 * i + q + 1)
                    if not isinstance(i, int) or i >= 1:
                        dve.wait_ge(hhi_ready, 2 * i + q - 1)
                        dve.wait_ge(hlo_ready, 2 * i + q - 1)
                    bias = b1_s[:, bass.ds(e, 1), q * 4:q * 4 + 4].rearrange("p o k -> p (o k)").unsqueeze(2).to_broadcast([P, 4, P])
                    v.tensor_tensor(act_f[:, q * 512:(q + 1) * 512].rearrange("p (k n) -> p k n", k=4),
                                    ps_h[b][q].rearrange("p (k n) -> p k n", k=4), bias, ALU.add).then_inc(h_sum, 1)

            def h_lo(i, b):
                for q in range(2):
                    dve.wait_ge(hhi_ready, 2 * i + q + 1)
                    v.scalar_tensor_tensor(hT[:, b, 1, q * 512:(q + 1) * 512], act_f[:, q * 512:(q + 1) * 512], 0.0,
                                           hT[:, b, 0, q * 512:(q + 1) * 512], ALU.max, ALU.subtract).then_inc(hlo_ready, 1)

            def y_out(i, b):
                dve.wait_ge(y_ps, i + 1)
                dve.wait_ge(res_ready, i + 1)
                v.scalar_tensor_tensor(res[:, b, :], ps_y[b], 1.0 / (WSCALE * WSCALE), res[:, b, :],
                                       ALU.mult, ALU.add).then_inc(y_ready, 1)

            w1_copy(0, 0)
            x_lo(0, 0)

            def tile(i, b, first=False, last=False):
                if not last:
                    w1_copy(i + 1, 1 - b)
                add_b1(i, b)
                if not last:
                    x_lo(i + 1, 1 - b)
                h_lo(i, b)
                if not first:
                    y_out(i - 1, 1 - b)

            tile(0, 0, first=True)
            tile(1, 1)
            with dve.Fori(1, (SLOT_TILES - 1) // 2) as j:
                tile(2 * j, 0)
                tile(2 * j + 1, 1)
            tile(SLOT_TILES - 1, (SLOT_TILES - 1) % 2, last=True)
            y_out(SLOT_TILES - 1, (SLOT_TILES - 1) % 2)

        @block.tensor
        def _(pe):
            t_ = nc.tensor
            for n in range(G):
                pe.wait_ge(diag_ready, n + 1)
                if n % 2 == 0:
                    pe.wait_ge(ld_cw[n // 2], 16)
                last = t_.matmul(ps_cond, diag[:, n, :], condw[:, n, :], start=(n == 0), stop=(n == G - 1))
            last.then_inc(cond_ps, 1)
            pe.wait_ge(ld_small, 64)
            pe.wait_ge(bias_ready, 2)
            for b in range(B):
                pe.wait_ge(wbot_ready, b + 1)
                for kt in range(KD):
                    for ko in range(KD):
                        last = t_.transpose(ps_wT[b][:, kt * D + ko * P:kt * D + ko * P + P],
                                            wbot[:, b, ko, kt * P:kt * P + P], ident[:, :])
                last.then_inc(wT_ps, 1)
            for b in range(B):
                for kt in range(KD):
                    at = (b * KD + kt) * E
                    for ko in range(KD):
                        t_.matmul(ps_gate[:, at:at + E], wbot[:, b, ko, kt * P:kt * P + P], gate[:, ko, :],
                                  start=(ko == 0), stop=(ko == KD - 1))
            for ko in range(KD):
                last = t_.matmul(ps_gate[:, 2 * KD * E:], bias_mat[:, ko, :], gate[:, ko, :],
                                 start=(ko == 0), stop=(ko == KD - 1))
            last.then_inc(gate_ps, 1)
            pe.wait_ge(rhs_ready, 1)
            for t in range(TT):
                b = t // TPB
                if t % TPB == 0:
                    pe.wait_ge(ld_x[b], 16)
                    pe.wait_ge(wT_ready, b + 1)
                if t >= 4:
                    pe.wait_ge(rows_ready, t - 3)
                for k in range(KD):
                    last = t_.matmul(ps_rows[t % 4], xT[:, k, t * P:(t + 1) * P], rhs[:, b, k, :],
                                     start=(k == 0), stop=(k == KD - 1))
                last.then_inc(rows_ps, 1)
            pe.wait_ge(oh_ready, 1)
            oh_f = oh[:, :, :].rearrange("p e t -> p (e t)")
            t_.matmul(ps_prefix, before[:, :], oh_f, start=True, stop=True)
            t_.matmul(ps_count, ones_h[:, :], oh_f, start=True, stop=True).then_inc(rank_ps, 1)
            for t in range(TT):
                pe.wait_ge(tok_rhs_ready, t + 2)
                last = t_.matmul(ps_tok, oh_slot[:, t, :], tok_rhs[:, t, :], start=(t == 0), stop=(t == TT - 1))
            last.then_inc(tok_ps, 1)

            pe.wait_ge(routed, 1)

            def transpose_x(i, b, turn):
                pe.wait_ge(x_in[b], 16 * turn)
                if not isinstance(i, int) or i >= 1:
                    pe.wait_ge(xlo_ready, i)
                for k in range(KD):
                    last = t_.transpose(ps_xT[:, k * P:(k + 1) * P], xg[:, b, k * P:(k + 1) * P], ident[:, :])
                last.then_inc(xT_ps, 1)

            def layer1(i, b):
                pe.wait_ge(w1_ready, i + 1)
                pe.wait_ge(xlo_ready, i + 1)
                if not isinstance(i, int) or i >= 2:
                    pe.wait_ge(h_sum, 2 * i - 2)
                for c in range(KH):
                    o = ps_h[b][c // 4][:, (c % 4) * P:(c % 4 + 1) * P]
                    for k in range(KD):
                        for wp, xp in ((0, 0), (0, 1), (1, 0)):
                            last = t_.matmul(o, w1s[:, b, wp, k * H + c * P:k * H + (c + 1) * P],
                                             xs[:, b, xp, k * P:(k + 1) * P],
                                             start=(k + wp + xp == 0), stop=(k == KD - 1 and wp == 1))
                    if c % 4 == 3:
                        last.then_inc(h_ps, 1)

            def layer2(i, b):
                e = pe.value_load(tile_expert[0:1, bass.ds(i, 1)], min_val=0, max_val=E - 1)
                pe.wait_ge(hlo_ready, 2 * i + 2)
                if not isinstance(i, int) or i >= 2:
                    pe.wait_ge(y_ready, i - 1)
                for c in range(KH):
                    for hp, wp in ((0, 0), (0, 1), (1, 0)):
                        last = t_.matmul(ps_y[b], hT[:, b, hp, c * P:(c + 1) * P],
                                         wsplit[:, bass.ds(e, 1), wp, W1E + c * D:W1E + (c + 1) * D].rearrange("p o n -> p (o n)"),
                                         start=(c + hp + wp == 0), stop=(c == KH - 1 and hp == 1))
                last.then_inc(y_ps, 1)

            transpose_x(0, 0, 1)
            layer1(0, 0)
            transpose_x(1, 1, 1)
            layer1(1, 1)
            transpose_x(2, 0, 2)
            layer2(0, 0)
            with pe.Fori(1, (SLOT_TILES - 1) // 2) as j:
                layer1(2 * j, 0)
                transpose_x(2 * j + 1, 1, j + 1)
                layer2(2 * j - 1, 1)
                layer1(2 * j + 1, 1)
                transpose_x(2 * j + 2, 0, j + 2)
                layer2(2 * j, 0)
            n = SLOT_TILES - 1
            layer1(n, n % 2)
            layer2(n - 1, 1 - n % 2)
            layer2(n, n % 2)


def kernel(x, cond_8, L0_cond_weight, L0_cond_mask, L0_cond_bias, L0_ffn_gate_w, L0_ffn_gate_b,
           L0_ffn_w1, L0_ffn_b1, L0_ffn_w2, L0_ffn_b2):
    import numpy as np
    import concourse.bacc as bacc
    from concourse.bass_utils import run_bass_kernel_spmd

    def c(a):
        return np.ascontiguousarray(a)

    x, y, cw, cm, cb, gw, gb, w1, b1, w2, b2 = map(np.asarray, (
        x, cond_8, L0_cond_weight, L0_cond_mask, L0_cond_bias, L0_ffn_gate_w, L0_ffn_gate_b,
        L0_ffn_w1, L0_ffn_b1, L0_ffn_w2, L0_ffn_b2))
    rows = x.reshape(TOK, D)
    w1_l = w1.transpose(0, 2, 1).reshape(E, KD, P, H).transpose(0, 2, 1, 3).reshape(E, P, W1E)
    w2_l = w2.transpose(0, 2, 1).reshape(E, KH, P, D).transpose(0, 2, 1, 3).reshape(E, P, W1E)
    arrays = {
        "x_t": c(rows.T.reshape(KD, P, TOK).transpose(1, 0, 2)),
        "x_rows": c(rows),
        "cond_y": c(y.reshape(B * G)),
        "cond_w": c(cw.reshape(4, 2, KD, P, D).transpose(0, 3, 1, 2, 4).reshape(4, P, 2, CW)),
        "cond_mask": c(cm.reshape(KD, P, D).transpose(1, 0, 2).reshape(P, CW)),
        "cond_bias": c(cb),
        "gate_t": c(gw.T.reshape(KD, P, E).transpose(1, 0, 2)),
        "gate_b": c(gb),
        "w_all": c(np.concatenate([w1_l, w2_l], axis=2)),
        "b1_t": c(b1.reshape(E, KH, P).transpose(2, 0, 1)),
        "b2": c(b2),
    }
    nc = bacc.Bacc("TRN2", target_bir_lowering=False, num_devices=1)
    args = [nc.dram_tensor(n, a.shape, mybir.dt.from_np(a.dtype), kind="ExternalInput").ap() for n, a in arrays.items()]
    out = nc.dram_tensor("out", (TOK, D), F32, kind="ExternalOutput").ap()
    build(nc, *args, out)
    r = run_bass_kernel_spmd(nc, [arrays], core_ids=[0])
    return r.results[0]["out"].reshape(B, S, D)
```

```python
from contextlib import ExitStack

import concourse.bass as bass
from concourse import mybir

ALU = mybir.AluOpType
ACT = mybir.ActivationFunctionType
AX = mybir.AxisListType
F32 = mybir.dt.float32
F16 = mybir.dt.float16
BF16 = mybir.dt.bfloat16
I32 = mybir.dt.int32

P = 128
B, S, D = 2, 1024, 256
E, H, G = 8, 1024, 8
TOK = B * S
TT = TOK // P
TPB = S // P
KD = D // P
KH = H // P
SLOT_TILES = TOK // P + E - 1
ST = SLOT_TILES + 1
NT = SLOT_TILES + 3
CW = KD * D
CH = 1024
CPL = D * H // P // CH
CPE = 2 * CPL
CHUNKS = E * CPE
AHEAD = 2
POOL_SPLITS = 4
LOADED = 2 * CPE
EARLY = 6
PER_PAIR, PER_FIRST = 4, 2
WSCALE = 64.0
RING = 4
HALF = KH * P // 2
SURE = TOK // P
LOOPS = (SURE - 2) // RING
AFTER = 2 + LOOPS * RING
STORES = ((0, 6), (6, 11), (11, 14), (14, 16))
B1_ROWS = 36
X16_PLACE = LOADED + AHEAD
XC = 512


def build(nc, x_t, x_rows, cond_y, cond_w, cond_mask, cond_bias, gate_t, gate_b, w_all, b1, b2, out):
    xf_rows = nc.dram_tensor("xf_rows", [TOK, D], F32, kind="Internal").ap()
    b1_scratch = nc.dram_tensor("b1_scratch", [2, E * KH, P], F16, kind="Internal").ap()
    with ExitStack() as ctx:
        def sb(name, shape, dt=F32):
            return ctx.enter_context(nc.sbuf_tensor(name, shape, dt))

        def sem(name):
            return ctx.enter_context(nc.semaphore(name))

        wsp = sb("wsp", [P, (CHUNKS + AHEAD) * 2 * CH], F16)

        def place32(n):
            return wsp[:, bass.ds(n * 2 * CH, 2 * CH)].bitcast(F32)

        def hi_of(n):
            return wsp[:, bass.ds(n * 2 * CH, CH)]

        def lo_of(n):
            return wsp[:, bass.ds(n * 2 * CH + CH, CH)]

        at = (CHUNKS + AHEAD - 2 * CPE) * 2 * CH
        condw = wsp[:, at:at + CPE * 2 * CH].bitcast(F32).rearrange("p (g n) -> p g n", g=G)
        at += CPE * 2 * CH
        xT = wsp[:, at:at + CPE * 2 * CH].bitcast(F32).rearrange("p (k n) -> p k n", k=KD)

        x16 = wsp[:, X16_PLACE * 2 * CH:(X16_PLACE + 4) * 2 * CH].rearrange("p (a k n) -> p a k n", a=2, k=KD)

        stage = sb("stage", [P, TT * D + 5 * CW])
        xf = stage[:, 0:TT * D].rearrange("p (t n) -> p t n", n=D)
        at = TT * D
        wbot = stage[:, at:at + 2 * CW].rearrange("p (b k n) -> p b k n", b=B, k=KD)
        oh_slot = stage[:, at:at + TT * P // 2].bitcast(BF16).rearrange("p (t n) -> p t n", t=TT)
        at += 2 * CW
        w_t = stage[:, at:at + 2 * CW].bitcast(F16).rearrange("p (b a n) -> p b a n", b=B, a=2)
        at += 2 * CW
        mask = stage[:, at:at + CW]
        w1s = stage[:, 0:2 * CPL * CH].bitcast(F16).rearrange("p (b n) -> p b n", b=2)
        w2s = stage[:, 2 * CPL * CH:3 * CPL * CH].bitcast(F16).rearrange("p (b n) -> p b n", b=2)

        hT = sb("hT", [P, 2, 2, KH * P], F16)
        products = hT[:, :, :, :].rearrange("p b a n -> p (b a n)").bitcast(F32).rearrange("p (r n) -> p r n", n=CW)
        logits_t = hT[0:E, :, :, :].rearrange("p b a n -> p (b a n)").bitcast(F32)
        b2_all = sb("b2_all", [P, E, D])
        y_all = sb("y_all", [P, B * G])
        gate = sb("gate", [P, KD, E])
        bias_col = sb("bias_col", [P, KD])
        gate_w = sb("gate_w", [P, B, KD * E])
        logit_bias = sb("logit_bias", [E, 1])
        gate_bias = sb("gate_bias", [E, 1])
        b1_parts = sb("b1_parts", [B1_ROWS, E, 2, P], F16)
        chunk_of = sb("chunk_of", [B1_ROWS, 4, P], F16)
        b1_raw = sb("b1_raw", [E * KH, P])
        b1_split = sb("b1_split", [E * KH, 2, P], F16)
        ident = sb("ident", [P, P])
        ones = sb("ones", [P, E * TT])
        before = sb("before", [P, P], BF16)
        ones_h = sb("ones_h", [P, P], BF16)
        iota_r = sb("iota_r", [P, P], BF16)
        e_less_8 = sb("e_less_8", [P, E])
        tile_no = sb("tile_no", [P, ST])
        tile_at = sb("tile_at", [P, NT])
        usual_goal = sb("usual_goal", [P, NT])
        tok_tile = sb("tok_tile", [P, TT])
        part_no = sb("part_no", [P, 1])

        best = sb("best", [P, TT])
        pick = sb("pick", [P, TT, E])
        first = sb("first", [P, TT])
        oh = sb("oh", [P, E, TT], BF16)
        count = sb("count", [P, E])
        per_tile = sb("per_tile", [P, E * TT])
        upto = sb("upto", [P, E, TT])
        padded_i = sb("padded_i", [P, 2, E], I32)
        padded = sb("padded", [P, E])
        ends = sb("ends", [P, E])
        offs = sb("offs", [P, 3, E])
        place = sb("place", [P, E, TT])
        slot_f = sb("slot_f", [P, TT])
        slot_i = sb("slot_i", [P, 3, TT], I32)
        slot_lo = sb("slot_lo", [P, TT])
        slot_hi = sb("slot_hi", [P, TT])
        sel = sb("sel", [P, TT, ST])
        tok_rhs = sb("tok_rhs", [P, TT, 2 * ST], BF16)
        tok_f = sb("tok_f", [P, 2 * ST])
        tok_sum = sb("tok_sum", [P, ST])
        tok_of_slot = sb("tok_of_slot", [P, ST], I32)
        past = sb("past", [P, NT, E])
        tile_e = sb("tile_e", [P, NT])
        goal_f = sb("goal_f", [P, 2, NT])
        same = sb("same", [P, NT])
        packed = sb("packed", [P, 4, ST])
        tile_expert = sb("tile_expert", [P, ST], I32)
        tile_plan = sb("tile_plan", [P, ST], I32)
        tiles_used = sb("tiles_used", [P, 2], I32)

        xg = sb("xg", [P, RING, D])
        res = sb("res", [P, RING, D])
        xs = sb("xs", [P, 2, 2, D], F16)

        psum = ctx.enter_context(nc.psum_tensor("psum", [P, 8, 512], F32))
        ps_prefix, ps_xT = psum[:, 0, 0:E * TT], psum[:, 0, 0:D]
        ps_wT = [psum[:, 1, :], psum[:, 2, :]]
        ps_gate = [psum[:, 3, 0:KD * E], psum[:, 0, 0:KD * E]]
        ps_gate_bias = psum[0:E, 7, 0:1]
        ps_logits_t = [psum[0:E, 4 + n, :] for n in range(TOK // XC)]
        ps_logits = psum[:, 3, 0:TT * E]
        ps_count, ps_tok = psum[:, 1, 0:E * TT], psum[:, 2, 0:2 * ST]
        ps_rows = [psum[:, 4 + n, 0:D] for n in range(4)]
        ps_h = [[psum[:, 1 + 2 * n + q, :] for q in range(2)] for n in range(2)]
        ps_y = [psum[:, 5 + n, 0:D] for n in range(2)]

        ld_y, ld_mask, ld_small, ld_b1, ld_b2 = map(sem, ["ld_y", "ld_mask", "ld_small", "ld_b1", "ld_b2"])
        ld_cw = [sem(f"ld_cw{n}") for n in range(4)]
        ld_x = [sem(f"ld_x{n}") for n in range(B)]
        ld_chunk = [sem(f"ld_chunk{n}") for n in range(CPE)]
        landed = sem("landed")
        consts = sem("consts")
        pool_step = sem("pool_step")
        product_ready = sem("product_ready")
        cond_sum = sem("cond_sum")
        raw_scaled = sem("raw_scaled")
        wbot0_ready = sem("wbot0_ready")
        wbot1_ready = sem("wbot1_ready")
        wT_ps = sem("wT_ps")
        wT_ready = sem("wT_ready")
        wT_lo_ready = sem("wT_lo_ready")
        x16_hi_ready = sem("x16_hi_ready")
        x16_lo_ready = [sem(f"x16_lo_ready{n}") for n in range(B)]
        b1_ready = sem("b1_ready")
        gate_ps = sem("gate_ps")
        gate_w_ready = sem("gate_w_ready")
        gate_bias_ps = sem("gate_bias_ps")
        logit_bias_ready = sem("logit_bias_ready")
        logits_t_ps = sem("logits_t_ps")
        logits_t_ready = sem("logits_t_ready")
        logits_ps = sem("logits_ps")
        rows_ps = sem("rows_ps")
        rows_ready = sem("rows_ready")
        rows_stored = [sem(f"rows_stored{n}") for n in range(len(STORES))]
        hi_ready = sem("hi_ready")
        lo_pool = sem("lo_pool")
        lo_dve = sem("lo_dve")
        lo_late = sem("lo_late")
        oh_ready = sem("oh_ready")
        rank_ps = sem("rank_ps")
        dve_step = sem("dve_step")
        tok_rhs_ready = sem("tok_rhs_ready")
        tok_ps = sem("tok_ps")
        experts_known = sem("experts_known")
        routed = sem("routed")
        x_in = [sem(f"x_in{n}") for n in range(RING)]
        res_in = [sem(f"res_in{n}") for n in range(RING)]
        stored = [sem(f"stored{n}") for n in range(RING)]
        res_ready = sem("res_ready")
        xT_ps = sem("xT_ps")
        xhi_ready = sem("xhi_ready")
        xlo_ready = sem("xlo_ready")
        w1_ready = sem("w1_ready")
        w2_ready = sem("w2_ready")
        h_ps = sem("h_ps")
        b1_high = sem("b1_high")
        b1_low = sem("b1_low")
        b1_stored = sem("b1_stored")
        hhi_ready = sem("hhi_ready")
        hlo_ready = sem("hlo_ready")
        y_ps = sem("y_ps")
        y_ready = sem("y_ready")

        N_CONST = 12
        RANKS_AFTER = 3
        HIGH_AFTER = (1, 6, 10)

        def late(i, n):
            return not isinstance(i, int) or i >= n

        class Plan:
            def __init__(self, eng, i):
                word = eng.value_load(tile_plan[0:1, bass.ds(i + 1, 1)], min_val=0, max_val=(1 << 18) - 1)
                self.expert, self.next_expert = word & 7, (word >> 3) & 7
                self.goal, self.next_goal = (word >> 6) & 31, (word >> 11) & 31
                self.same, self.next_same = (word >> 16) & 1, (word >> 17) & 1

        def following_plan(eng, i, plan):
            return None if isinstance(i, int) and i == SLOT_TILES - 1 else Plan(eng, i + 1)

        def split_chunks(eng, split, done, goal):
            more = goal - done
            with eng.If(more > 0):
                with eng.Fori(0, more) as m:
                    split(nc.s_assert_within(done + m, 0, CHUNKS - EARLY - 1, skip_runtime_bounds_check_because=
                                             "done + m < goal, which is at most CHUNKS - EARLY"))
            with eng.Else():
                eng.nop()

        def if_used(eng, used, i, work):
            if not isinstance(i, int) or i < SURE:
                work()
            elif i < SLOT_TILES:
                with eng.If(used > i):
                    work()
                with eng.Else():
                    eng.nop()

        def load_used(eng):
            return eng.value_load(tiles_used[0:1, 1:2], min_val=SURE, max_val=SLOT_TILES)

        def slot_tiles(eng, tile, plans=True):
            plan = tile(0, 0, 0, 1, plans and Plan(eng, 0))
            tile(1, 1, 1, 1, plan)
            with eng.Fori(0, LOOPS) as j:
                plan = plans and Plan(eng, RING * j + 2)
                for u in range(RING):
                    plan = tile(RING * j + 2 + u, u % 2, (2 + u) % RING, j + 1 + (2 + u) // RING, plan)
            plan = plans and Plan(eng, AFTER)
            for i in range(AFTER, SLOT_TILES):
                plan = tile(i, i % 2, i % RING, i // RING + 1, plan)

        block = ctx.enter_context(nc.Block())

        @block.sync
        def _(sp):
            sp.dma_start(y_all[:, :], cond_y.partition_broadcast(P)).then_inc(ld_y, 16)
            for n in range(4):
                sp.dma_start(condw[:, 2 * n:2 * n + 2, :], cond_w[n]).then_inc(ld_cw[n], 16)
                if n == 0:
                    sp.dma_start(mask, cond_mask).then_inc(ld_mask, 16)

            for b in range(B):
                sp.dma_start(xT[:, :, b * S:(b + 1) * S], x_t[:, :, b * S:(b + 1) * S]).then_inc(ld_x[b], 16)

            def load_chunk(e, q):
                src = w_all[bass.ds(e, 1), :, q * CH:(q + 1) * CH].rearrange("o p n -> (o p) n")
                sp.dma_start(place32(e * CPE + q + AHEAD), src).then_inc(ld_chunk[q], 16)

            def confirm(q, turn):
                sp.wait_ge(ld_chunk[q], 16 * turn)
                sp.sem_inc(landed, 1)

            def store_rows(n):
                t, end = STORES[n]
                sp.wait_ge(rows_ready, end)
                sp.dma_start(xf_rows[t * P:end * P, :].rearrange("(t p) d -> p t d", p=P),
                             xf[:, t:end, :]).then_inc(rows_stored[n], 16)

            for q in range(CPE):
                load_chunk(0, q)
            for e in range(1, LOADED // CPE):
                for q in range(CPE):
                    confirm(q, e)
                    load_chunk(e, q)
            sp.wait_ge(b1_low, 1)
            sp.dma_start(b1_scratch.rearrange("a r m -> r a m"), b1_split[:, :, :]).then_inc(b1_stored, 16)
            for q in range(CPE):
                confirm(q, LOADED // CPE)
            sp.wait_ge(consts, N_CONST)
            sp.wait_ge(b1_stored, 16)
            for part in range(2):
                sp.dma_start(b1_parts[32 * part:32 * part + 4, :, :, :],
                             b1_scratch[part].rearrange("(e q c) m -> c e q m", e=E, q=2)).then_inc(b1_ready, 16)
            for n in range(len(STORES)):
                store_rows(n)
            sp.dma_start(b2_all[:, :, :], b2.partition_broadcast(P)).then_inc(ld_b2, 16)
            sp.wait_ge(x_in[1], 16)
            sp.wait_ge(wbot0_ready, 1)
            sp.wait_ge(wbot1_ready, 1)
            sp.wait_ge(rows_ps, TT)
            sp.wait_ge(b1_ready, 32)
            for n in range(len(STORES)):
                sp.wait_ge(rows_stored[n], 16)
            load_chunk(LOADED // CPE, 0)
            load_chunk(LOADED // CPE, 1)
            with sp.Fori(LOADED // CPE, E - 1) as e:
                for q in range(CPE):
                    confirm(q, e + 1)
                    load_chunk(e + (q + 2) // CPE, (q + 2) % CPE)
            for q in range(CPE):
                confirm(q, E)
                if q + 2 < CPE:
                    load_chunk(E - 1, q + 2)

        @block.gpsimd
        def _(pool):
            g = nc.gpsimd
            g.memset(ident[:, :], 0.0).then_inc(pool_step, 1)
            g.memset(ones_h[:, :], 1.0).then_inc(pool_step, 1)
            pool.wait_ge(pool_step, 2)
            g.affine_select(out=ident[:, :], in_=ident[:, :], compare_op=ALU.not_equal, fill=1.0, base=0,
                            pattern=[[-1, P]], channel_multiplier=1).then_inc(consts, 1)
            g.memset(ones[:, :], 1.0).then_inc(consts, 1)
            g.memset(b1_parts[:, :, :, :], 0.0).then_inc(consts, 1)
            g.memset(chunk_of[:, :, :], 0.0).then_inc(pool_step, 1)
            for n, row in enumerate((0, 32)):
                pool.wait_ge(pool_step, n + 3)
                g.affine_select(out=chunk_of[row:row + 4, :, :], in_=chunk_of[row:row + 4, :, :],
                                compare_op=ALU.not_equal, fill=1.0, base=0, pattern=[[-1, 4], [0, P]],
                                channel_multiplier=1).then_inc(pool_step, 1)
            pool.wait_ge(pool_step, 5)
            acc = wbot[:, 1, :, :].rearrange("p k n -> p (k n)")
            for n in range(1, 4):
                pool.wait_ge(product_ready, n + 1)
                g.tensor_tensor(acc, products[:, 0, :] if n == 1 else acc, products[:, n, :], ALU.add).then_inc(cond_sum, 1)
                pool.wait_ge(cond_sum, n)
            g.affine_select(out=before[:, :], in_=ones_h[:, :], compare_op=ALU.is_gt, fill=0.0, base=0,
                            pattern=[[1, P]], channel_multiplier=-1).then_inc(consts, 1)

            def iota(t, pattern, base=0, cm=0):
                g.iota(t, pattern, base=base, channel_multiplier=cm,
                       allow_small_or_imprecise_dtypes=True).then_inc(consts, 1)

            iota(iota_r[:, :], [[1, P]])
            iota(e_less_8[:, :], [[1, E]], base=-E)
            iota(tile_no[:, :], [[1, ST]])
            iota(tile_at[:, :], [[P, NT]], base=-P)
            iota(tok_tile[:, :], [[1, TT]], base=-TT)
            iota(part_no[:, :], [[0, 1]], cm=1)
            iota(usual_goal[:, :], [[PER_PAIR, NT // 2], [PER_FIRST, 2]], base=-PER_FIRST)
            g.memset(same[:, :], 0.0).then_inc(consts, 1)
            g.memset(xg[:, :, :], 0.0).then_inc(pool_step, 1)
            g.memset(res[:, :, :], 0.0).then_inc(pool_step, 1)

            pool.wait_ge(x16_hi_ready, 1)
            g.tensor_tensor(x16[:, 1, :, 0:S], xT[:, :, 0:S], x16[:, 0, :, 0:S], ALU.subtract).then_inc(x16_lo_ready[0], 1)
            for n in range(POOL_SPLITS):
                pool.wait_ge(hi_ready, n + 1)
                raw = place32(n + AHEAD)
                g.tensor_scalar(raw, raw, WSCALE, 1.0, ALU.mult, ALU.mult).then_inc(raw_scaled, 1)
                pool.wait_ge(raw_scaled, n + 1)
                g.tensor_tensor(lo_of(n), raw, hi_of(n), ALU.subtract).then_inc(lo_pool if n < EARLY - AHEAD else lo_late, 1)

            def token(i):
                return bass.IndirectOffsetOnAxis(ap=tok_of_slot[:, i:i + 1], axis=0)

            def gather_x(i):
                if i >= RING:
                    pool.wait_ge(xT_ps, i - RING + 1)
                g.indirect_dma_start(xg[:, i % RING, :], None, xf_rows, token(i),
                                     bounds_check=TOK - 1, oob_is_err=False).then_inc(x_in[i % RING], 16)

            def gather_res(i):
                if i >= RING:
                    pool.wait_ge(stored[i % RING], 16 * (i // RING))
                g.indirect_dma_start(res[:, i % RING, :], None, x_rows, token(i),
                                     bounds_check=TOK - 1, oob_is_err=False).then_inc(res_in[i % RING], 16)

            def add_b2(i):
                e = pool.value_load(tile_expert[0:1, i:i + 1], min_val=0, max_val=E - 1)
                pool.wait_ge(res_in[i % RING], 16 * (i // RING + 1))
                g.tensor_tensor(res[:, i % RING, :], res[:, i % RING, :],
                                b2_all[:, bass.ds(e, 1), :].rearrange("p a n -> p (a n)"), ALU.add).then_inc(res_ready, 1)

            def scatter(i):
                pool.wait_ge(y_ready, i + 1)
                g.indirect_dma_start(out, token(i), res[:, i % RING, :], None,
                                     bounds_check=TOK - 1, oob_is_err=False).then_inc(stored[i % RING], 16)

            pool.wait_ge(pool_step, 7)
            for n in range(len(STORES)):
                pool.wait_ge(rows_stored[n], 16)
            pool.wait_ge(routed, 1)
            for i in range(RING):
                gather_x(i)
            gather_res(0)
            pool.wait_ge(ld_b2, 16)
            pool.wait_ge(experts_known, 1)
            used = load_used(pool)
            for i in range(SLOT_TILES + 2):
                if_used(pool, used, i + RING, lambda: gather_x(i + RING))
                if_used(pool, used, i + 1, lambda: gather_res(i + 1))
                if_used(pool, used, i, lambda: add_b2(i))
                if i >= 2:
                    if_used(pool, used, i - 2, lambda: scatter(i - 2))
            for i in range(SURE - RING, SLOT_TILES):
                if_used(pool, used, i, lambda: pool.wait_ge(stored[i % RING], 16 * (i // RING + 1)))

        @block.scalar
        def _(act):
            a = nc.scalar
            act.dma_start(gate[:, :, :], gate_t).then_inc(ld_small, 16)
            act.dma_start(bias_col[:, :], cond_bias.rearrange("(k p) -> p k", p=P),
                          allow_slow_non_contiguous=True).then_inc(ld_small, 16)
            act.dma_start(b1_raw[:, :], b1).then_inc(ld_b1, 16)
            act.dma_start(gate_bias[:, :], gate_b.rearrange("(e o) -> e o", o=1),
                          allow_slow_non_contiguous=True).then_inc(ld_small, 16)
            act.wait_ge(ld_b1, 16)
            a.mul(b1_split[:, 0, :], b1_raw[:, :], WSCALE).then_inc(b1_high, 1)
            act.wait_ge(ld_y, 16)
            for n in range(4):
                if n % 2 == 0:
                    act.wait_ge(ld_cw[n // 2], 16)
                a.mul(products[:, n, :], condw[:, n, :], y_all[:, G + n:G + n + 1]).then_inc(product_ready, 1)

            def high(n):
                act.wait_ge(landed, n + 1)
                if n >= POOL_SPLITS + AHEAD:
                    act.wait_ge(lo_dve, n - AHEAD + 1 - POOL_SPLITS)
                elif n >= AHEAD:
                    act.wait_ge(lo_pool, n - AHEAD + 1)
                a.mul(hi_of(n), place32(n + AHEAD), WSCALE).then_inc(hi_ready, 1)

            def x_high(b):
                act.wait_ge(ld_x[b], 16)
                a.copy(x16[:, 0, :, b * S:(b + 1) * S], xT[:, :, b * S:(b + 1) * S]).then_inc(x16_hi_ready, 1)

            def gate_w_out(b):
                act.wait_ge(gate_ps, b + 1)
                a.copy(gate_w[:, b, :], ps_gate[b]).then_inc(gate_w_ready, 1)

            def w_t_out(b):
                act.wait_ge(wT_ps, b + 1)
                a.mul(w_t[:, b, 0, :], ps_wT[b], WSCALE).then_inc(wT_ready, 1)

            def high(n):
                act.wait_ge(landed, n + 1)
                if n >= POOL_SPLITS + AHEAD:
                    act.wait_ge(lo_dve, n - AHEAD + 1 - POOL_SPLITS)
                elif n >= AHEAD:
                    act.wait_ge(lo_pool, n - AHEAD + 1)
                a.mul(hi_of(n), place32(n + AHEAD), WSCALE).then_inc(hi_ready, 1)

            gate_w_out(0)
            act.wait_ge(ld_small, 48)
            act.wait_ge(gate_bias_ps, 1)
            a.activation(logit_bias[:, :], ps_gate_bias, ACT.Identity, bias=gate_bias[:, 0:1]).then_inc(logit_bias_ready, 1)
            x_high(0)
            w_t_out(0)
            x_high(1)
            gate_w_out(1)
            high(0)
            w_t_out(1)
            high(1)

            for t in range(TT):
                act.wait_ge(rows_ps, t + 1)
                a.mul(xf[:, t, :], ps_rows[t % 4], 1.0 / WSCALE).then_inc(rows_ready, 1)
                if t in HIGH_AFTER:
                    high(B + HIGH_AFTER.index(t))

            def high_late(m):
                act.wait_ge(landed, m + EARLY + 1)
                act.wait_ge(lo_late, m + 1)
                a.mul(hi_of(m + EARLY), place32(m + EARLY + AHEAD), WSCALE).then_inc(hi_ready, 1)

            for n in range(B + len(HIGH_AFTER), EARLY):
                high(n)
            act.wait_ge(experts_known, 1)

            def w2_copy(i, b, plan):
                act.wait_ge(hi_ready, plan.goal + EARLY)
                if late(i, 2):
                    act.wait_ge(y_ps, i - 1)
                src = wsp[:, bass.ds(plan.expert * (CPE * 2 * CH) + CPL * 2 * CH, CPL * 2 * CH)].rearrange(
                    "p (c a n) -> p c a n", c=CPL, a=2)[:, :, 0, :]

                def copy():
                    a.copy(w2s[:, b, :].rearrange("p (c n) -> p c n", c=CPL), src).then_inc(w2_ready, 1)

                if late(i, 2):
                    with act.If(plan.same == 0):
                        copy()
                    with act.Else():
                        act.wait_ge(w2_ready, i)
                        act.nop().then_inc(w2_ready, 1)
                else:
                    copy()

            def x_hi(i, b):
                act.wait_ge(xT_ps, i + 1)
                if late(i, 2):
                    act.wait_ge(h_ps, 2 * i - 2)
                for k in range(KD):
                    last = a.activation(xs[:, b, 0, k * P:(k + 1) * P], ps_xT[:, k * P:(k + 1) * P], ACT.Identity,
                                        bias=bias_col[:, k:k + 1])
                last.then_inc(xhi_ready, 1)

            def h_hi(i, b):
                if late(i, 2):
                    act.wait_ge(y_ps, i - 1)
                for q in range(2):
                    act.wait_ge(h_ps, 2 * i + q + 1)
                    a.activation(hT[:, b, 0, q * HALF:(q + 1) * HALF], ps_h[b][q], ACT.Relu).then_inc(hhi_ready, 1)

            used = load_used(act)
            plan = Plan(act, -1)
            split_chunks(act, high_late, 0, plan.goal)
            x_hi(0, 0)
            split_chunks(act, high_late, plan.goal, plan.next_goal)

            def tile(i, b, r, turn, plan):
                if_used(act, used, i + 1, lambda: x_hi(i + 1, 1 - b))
                if_used(act, used, i + 2, lambda: split_chunks(act, high_late, plan.goal, plan.next_goal))
                next_plan = following_plan(act, i, plan)
                if_used(act, used, i, lambda: w2_copy(i, b, plan))
                if_used(act, used, i, lambda: h_hi(i, b))
                return next_plan

            slot_tiles(act, tile)

        @block.vector
        def _(dve):
            v = nc.vector
            step = [0]

            def then(ins):
                ins.then_inc(dve_step, 1)
                step[0] += 1
                dve.wait_ge(dve_step, step[0])

            dve.wait_ge(ld_y, 16)
            acc = wbot[:, 0, :, :].rearrange("p k n -> p (k n)")
            for n in range(G):
                if n % 2 == 0:
                    dve.wait_ge(ld_cw[n // 2], 16)
                if n == 0:
                    then(v.tensor_scalar(acc, condw[:, 0, :], y_all[:, 0:1], None, ALU.mult))
                else:
                    then(v.scalar_tensor_tensor(acc, condw[:, n, :], y_all[:, n:n + 1], acc, ALU.mult, ALU.add))
            dve.wait_ge(ld_mask, 16)
            v.tensor_tensor(acc, acc, mask, ALU.mult).then_inc(wbot0_ready, 1)
            acc = wbot[:, 1, :, :].rearrange("p k n -> p (k n)")
            dve.wait_ge(cond_sum, 3)
            for n in range(4, G):
                then(v.scalar_tensor_tensor(acc, condw[:, n, :], y_all[:, G + n:G + n + 1], acc, ALU.mult, ALU.add))
            v.tensor_tensor(acc, acc, mask, ALU.mult).then_inc(wbot1_ready, 1)
            def logits_t_out(n):
                dve.wait_ge(logits_t_ps, n + 1)
                v.tensor_scalar(logits_t[:, n * XC:(n + 1) * XC], ps_logits_t[n], logit_bias[:, 0:1], None,
                                ALU.add).then_inc(logits_t_ready, 1)

            def w_t_low(b):
                dve.wait_ge(wT_ready, b + 1)
                v.scalar_tensor_tensor(w_t[:, b, 1, :], ps_wT[b], WSCALE, w_t[:, b, 0, :],
                                       ALU.mult, ALU.subtract).then_inc(wT_lo_ready, 1)

            dve.wait_ge(b1_high, 1)
            v.scalar_tensor_tensor(b1_split[:, 1, :], b1_raw[:, :], WSCALE, b1_split[:, 0, :],
                                   ALU.mult, ALU.subtract).then_inc(b1_low, 1)
            dve.wait_ge(logit_bias_ready, 1)
            logits_t_out(0)
            logits_t_out(1)
            w_t_low(0)
            dve.wait_ge(x16_hi_ready, 2)
            v.tensor_tensor(x16[:, 1, :, S:2 * S], xT[:, :, S:2 * S], x16[:, 0, :, S:2 * S],
                            ALU.subtract).then_inc(x16_lo_ready[1], 1)
            logits_t_out(2)
            w_t_low(1)
            logits_t_out(3)

            def low(n):
                dve.wait_ge(hi_ready, n + 1)
                v.scalar_tensor_tensor(lo_of(n), place32(n + AHEAD), WSCALE, hi_of(n),
                                       ALU.mult, ALU.subtract).then_inc(lo_dve if n < EARLY - AHEAD else lo_late, 1)

            def low_late(m):
                dve.wait_ge(hi_ready, m + EARLY + 1)
                v.scalar_tensor_tensor(lo_of(m + EARLY), place32(m + EARLY + AHEAD), WSCALE, hi_of(m + EARLY),
                                       ALU.mult, ALU.subtract).then_inc(lo_late, 1)

            def over_e(t):
                return t.unsqueeze(2).to_broadcast([P, TT, E])

            e_bc = e_less_8[:, :].unsqueeze(1).to_broadcast([P, TT, E])
            dve.wait_ge(logits_ps, 1)
            logits = ps_logits.rearrange("p (t e) -> p t e", e=E)
            dve.wait_ge(consts, N_CONST)
            then(v.tensor_reduce(best[:, :], logits, AX.X, ALU.max))
            then(v.tensor_tensor(pick[:, :, :], logits, over_e(best[:, :]), ALU.is_equal))
            then(v.tensor_tensor(pick[:, :, :], pick[:, :, :], e_bc, ALU.mult))
            then(v.tensor_reduce(first[:, :], pick[:, :, :], AX.X, ALU.min))
            v.tensor_tensor(oh[:, :, :].rearrange("p e t -> p t e"), e_bc, over_e(first[:, :]),
                            ALU.is_equal).then_inc(oh_ready, 1)

            dve.wait_ge(rank_ps, 1)
            then(v.tensor_copy(per_tile[:, :], ps_count))
            v.tensor_reduce(count[:, :], per_tile[:, :].rearrange("p (e t) -> p e t", e=E), AX.X, ALU.add)
            upto_f = upto[:, :, :].rearrange("p e t -> p (e t)")
            then(v.tensor_tensor_scan(upto_f, ones[:, 0:E * TT], per_tile[:, :], 0.0, ALU.mult, ALU.add))
            then(v.tensor_scalar(padded_i[:, 0, :], count[:, :], float(P - 1), None, ALU.add))
            then(v.tensor_scalar(padded_i[:, 1, :], padded_i[:, 0, :], -P, None, ALU.bitwise_and))
            then(v.tensor_copy(padded[:, :], padded_i[:, 1, :]))
            v.tensor_tensor(offs[:, 1, :], upto[:, :, TT - 1], count[:, :], ALU.subtract)
            then(v.tensor_tensor_scan(ends[:, :], ones[:, 0:E], padded[:, :], 0.0, ALU.mult, ALU.add))
            then(v.tensor_tensor(offs[:, 0, :], ends[:, :], padded[:, :], ALU.subtract))
            then(v.tensor_tensor(offs[:, 2, :], offs[:, 0, :], offs[:, 1, :], ALU.subtract))
            place_f = place[:, :, :].rearrange("p e t -> p (e t)")
            then(v.tensor_tensor(place_f, upto_f, per_tile[:, :], ALU.subtract))
            then(v.tensor_tensor(place_f, ps_prefix, place_f, ALU.add))
            then(v.tensor_tensor(place[:, :, :], place[:, :, :], offs[:, 2, :].unsqueeze(2).to_broadcast([P, E, TT]), ALU.add))
            then(v.tensor_tensor(place[:, :, :], place[:, :, :], oh[:, :, :], ALU.mult))
            then(v.tensor_reduce(slot_f[:, :], place[:, :, :].rearrange("p e t -> p t e"), AX.X, ALU.add))
            then(v.tensor_copy(slot_i[:, 0, :], slot_f[:, :]))
            v.tensor_scalar(slot_i[:, 1, :], slot_i[:, 0, :], P - 1, None, ALU.bitwise_and)
            then(v.tensor_scalar(slot_i[:, 2, :], slot_i[:, 0, :], 7, None, ALU.logical_shift_right))
            v.tensor_copy(slot_lo[:, :], slot_i[:, 1, :])
            then(v.tensor_copy(slot_hi[:, :], slot_i[:, 2, :]))
            then(v.tensor_tensor(sel[:, :, :], tile_no[:, :].unsqueeze(1).to_broadcast([P, TT, ST]),
                                 slot_hi[:, :].unsqueeze(2).to_broadcast([P, TT, ST]), ALU.is_equal))
            v.tensor_scalar(tok_rhs[:, :, 0:ST], sel[:, :, :], part_no[:, 0:1], None, ALU.mult)
            v.tensor_tensor(tok_rhs[:, :, ST:2 * ST], sel[:, :, :],
                            tok_tile[:, :].unsqueeze(2).to_broadcast([P, TT, ST]), ALU.mult).then_inc(tok_rhs_ready, 1)
            for t in range(TT):
                v.tensor_scalar(oh_slot[:, t, :], iota_r[:, :], slot_lo[:, t:t + 1], None, ALU.is_equal).then_inc(tok_rhs_ready, 1)
            low(POOL_SPLITS)
            dve.wait_ge(tok_ps, 1)
            then(v.tensor_copy(tok_f[:, :], ps_tok))
            then(v.scalar_tensor_tensor(tok_sum[:, :], tok_f[:, ST:2 * ST], float(P), tok_f[:, 0:ST], ALU.mult, ALU.add))
            v.tensor_scalar(tok_of_slot[:, :], tok_sum[:, :], float(TOK), None, ALU.add).then_inc(routed, 1)
            then(v.tensor_tensor(past[:, :, :], ends[:, :].unsqueeze(1).to_broadcast([P, NT, E]),
                                 tile_at[:, :].unsqueeze(2).to_broadcast([P, NT, E]), ALU.is_le))
            then(v.tensor_reduce(tile_e[:, :], past[:, :, :], AX.X, ALU.add))
            then(v.tensor_scalar(tile_e[:, :], tile_e[:, :], float(E - 1), None, ALU.min))
            v.tensor_copy(tile_expert[:, :], tile_e[:, 1:1 + ST])
            then(v.tensor_scalar(goal_f[:, 0, :], tile_e[:, :], float(CPE), float(CPE - EARLY), ALU.mult, ALU.add))
            then(v.tensor_tensor(goal_f[:, 0, :], goal_f[:, 0, :], usual_goal[:, :], ALU.max))
            then(v.tensor_scalar(goal_f[:, 1, :], goal_f[:, 0, :], float(CHUNKS - EARLY), 0.0, ALU.min, ALU.max))
            v.tensor_tensor(same[:, 2:NT], tile_e[:, 2:NT], tile_e[:, 0:NT - 2], ALU.is_equal)
            then(v.tensor_scalar(tiles_used[:, 0:1], ends[:, E - 1:E], 1.0, None, ALU.mult))
            v.tensor_scalar(tiles_used[:, 1:2], tiles_used[:, 0:1], 7, None, ALU.logical_shift_right)
            v.scalar_tensor_tensor(packed[:, 0, :], tile_e[:, 1:1 + ST], 8.0, tile_e[:, 0:ST], ALU.mult, ALU.add)
            then(v.scalar_tensor_tensor(packed[:, 1, :], goal_f[:, 1, 2:2 + ST], 32.0, goal_f[:, 1, 1:1 + ST], ALU.mult, ALU.add))
            v.scalar_tensor_tensor(packed[:, 2, :], packed[:, 1, :], 64.0, packed[:, 0, :], ALU.mult, ALU.add)
            then(v.scalar_tensor_tensor(packed[:, 3, :], same[:, 1:1 + ST], 2.0, same[:, 0:ST], ALU.mult, ALU.add))
            then(v.scalar_tensor_tensor(tile_plan[:, :], packed[:, 3, :], 65536.0, packed[:, 2, :], ALU.mult, ALU.add))
            v.nop().then_inc(experts_known, 1)
            for n in range(POOL_SPLITS + 1, EARLY):
                low(n)

            dve.wait_ge(lo_pool, min(POOL_SPLITS, EARLY - AHEAD))
            dve.wait_ge(experts_known, 1)
            dve.wait_ge(routed, 1)
            for n in range(len(STORES)):
                dve.wait_ge(rows_stored[n], 16)
            dve.wait_ge(tok_ps, 1)

            def w1_copy(i, b, plan):
                dve.wait_ge(lo_late, plan.goal + AHEAD)
                if late(i, 2):
                    dve.wait_ge(h_ps, 2 * i - 2)

                def copy():
                    v.tensor_copy(w1s[:, b, :], wsp[:, bass.ds(plan.next_expert * (CPE * 2 * CH), CPL * 2 * CH)]).then_inc(w1_ready, 1)

                if late(i, 2):
                    with dve.If(plan.next_same == 0):
                        copy()
                    with dve.Else():
                        dve.wait_ge(w1_ready, i)
                        dve.nop().then_inc(w1_ready, 1)
                else:
                    copy()

            def x_lo(i, b):
                dve.wait_ge(xhi_ready, i + 1)
                for k in range(KD):
                    last = v.scalar_tensor_tensor(xs[:, b, 1, k * P:(k + 1) * P], ps_xT[:, k * P:(k + 1) * P],
                                                  bias_col[:, k:k + 1], xs[:, b, 0, k * P:(k + 1) * P],
                                                  ALU.add, ALU.subtract)
                last.then_inc(xlo_ready, 1)

            def h_lo(i, b):
                for q in range(2):
                    dve.wait_ge(hhi_ready, 2 * i + q + 1)
                    v.scalar_tensor_tensor(hT[:, b, 1, q * HALF:(q + 1) * HALF], ps_h[b][q], 0.0,
                                           hT[:, b, 0, q * HALF:(q + 1) * HALF], ALU.max, ALU.subtract).then_inc(hlo_ready, 1)

            def y_out(i, b, r):
                dve.wait_ge(y_ps, i + 1)
                dve.wait_ge(res_ready, i + 1)
                v.scalar_tensor_tensor(res[:, r, :], ps_y[b], 1.0 / (WSCALE * WSCALE), res[:, r, :],
                                       ALU.mult, ALU.add).then_inc(y_ready, 1)

            used = load_used(dve)
            plan = Plan(dve, -1)
            split_chunks(dve, low_late, 0, plan.goal)
            w1_copy(0, 0, plan)
            x_lo(0, 0)
            split_chunks(dve, low_late, plan.goal, plan.next_goal)

            def tile(i, b, r, turn, plan):
                if_used(dve, used, i + 1, lambda: w1_copy(i + 1, 1 - b, plan))
                if_used(dve, used, i + 1, lambda: x_lo(i + 1, 1 - b))
                if late(i, 2):
                    if_used(dve, used, i - 2, lambda: y_out(i - 2, b, (r - 2) % RING))
                if_used(dve, used, i + 2, lambda: split_chunks(dve, low_late, plan.goal, plan.next_goal))
                next_plan = following_plan(dve, i, plan)
                if_used(dve, used, i, lambda: h_lo(i, b))
                return next_plan

            slot_tiles(dve, tile)
            for i in (SLOT_TILES - 2, SLOT_TILES - 1):
                if_used(dve, used, i, lambda: y_out(i, i % 2, i % RING))

        @block.tensor
        def _(pe):
            t_ = nc.tensor

            def turn_w(b):
                pe.wait_ge([wbot0_ready, wbot1_ready][b], 1)
                for kt in range(KD):
                    for ko in range(KD):
                        last = t_.transpose(ps_wT[b][:, kt * D + ko * P:kt * D + ko * P + P],
                                            wbot[:, b, ko, kt * P:kt * P + P], ident[:, :])
                last.then_inc(wT_ps, 1)

            def fold_gate(b):
                for kt in range(KD):
                    for ko in range(KD):
                        last = t_.matmul(ps_gate[b][:, kt * E:(kt + 1) * E], wbot[:, b, ko, kt * P:kt * P + P],
                                         gate[:, ko, :], start=(ko == 0), stop=(ko == KD - 1))
                last.then_inc(gate_ps, 1)

            def rows(t):
                b = t // TPB
                if t % TPB == 0:
                    pe.wait_ge(wT_ready, b + 1)
                    pe.wait_ge(wT_lo_ready, b + 1)
                    pe.wait_ge(x16_lo_ready[b], 1)
                if t >= 4:
                    pe.wait_ge(rows_ready, t - 3)
                for k in range(KD):
                    for xp, wp in ((0, 0), (0, 1), (1, 0)):
                        last = t_.matmul(ps_rows[t % 4], x16[:, xp, k, t * P:(t + 1) * P],
                                         w_t[:, b, wp, k * D:(k + 1) * D], start=(k + xp + wp == 0),
                                         stop=(k == KD - 1 and xp == 1))
                last.then_inc(rows_ps, 1)

            def gate_logits(b):
                pe.wait_ge(ld_x[b], 16)
                pe.wait_ge(gate_w_ready, b + 1)
                for n in range(b * S // XC, (b + 1) * S // XC):
                    for k in range(KD):
                        last = t_.matmul(ps_logits_t[n], gate_w[:, b, k * E:(k + 1) * E], xT[:, k, n * XC:(n + 1) * XC],
                                         start=(k == 0), stop=(k == KD - 1))
                    last.then_inc(logits_t_ps, 1)

            def turn_logits(n):
                pe.wait_ge(logits_t_ready, n + 1)
                for t in range(n * XC // P, (n + 1) * XC // P):
                    last = t_.transpose(ps_logits[:, t * E:(t + 1) * E], logits_t[:, t * P:(t + 1) * P], ident[0:E, 0:E])
                return last

            def keep_clock_up(n):
                for _ in range(n):
                    t_.matmul(psum[:, 6, :], ones_h[:, :], ones_h[:, :].unsqueeze(1).to_broadcast([P, 4, P]),
                              start=True, stop=True)

            pe.wait_ge(consts, 2)
            pe.wait_ge(ld_cw[2], 16)
            keep_clock_up(10)
            pe.wait_ge(ld_small, 48)
            pe.wait_ge(wbot0_ready, 1)
            fold_gate(0)
            turn_w(0)
            for ko in range(KD):
                last = t_.matmul(ps_gate_bias, gate[:, ko, :], bias_col[:, ko:ko + 1], start=(ko == 0), stop=(ko == KD - 1))
            last.then_inc(gate_bias_ps, 1)
            gate_logits(0)
            pe.wait_ge(wbot1_ready, 1)
            fold_gate(1)
            turn_w(1)
            pe.wait_ge(logit_bias_ready, 1)
            gate_logits(1)
            for n in range(TOK // XC):
                last = turn_logits(n)
            last.then_inc(logits_ps, 1)
            for t in range(RANKS_AFTER):
                rows(t)
            pe.wait_ge(oh_ready, 1)
            pe.wait_ge(consts, N_CONST)
            oh_f = oh[:, :, :].rearrange("p e t -> p (e t)")
            t_.matmul(ps_prefix, before[:, :], oh_f, start=True, stop=True)
            t_.matmul(ps_count, ones_h[:, :], oh_f, start=True, stop=True).then_inc(rank_ps, 1)
            for t in range(RANKS_AFTER, TT):
                rows(t)
            for t in range(TT):
                pe.wait_ge(tok_rhs_ready, t + 2)
                last = t_.matmul(ps_tok, oh_slot[:, t, :], tok_rhs[:, t, :], start=(t == 0), stop=(t == TT - 1))
            last.then_inc(tok_ps, 1)

            pe.wait_ge(routed, 1)
            pe.wait_ge(rows_ready, TT)
            pe.wait_ge(experts_known, 1)
            pe.wait_ge(b1_ready, 32)


            def turn_x(i, b, r, turn):
                pe.wait_ge(x_in[r], 16 * turn)
                if late(i, 1):
                    pe.wait_ge(xlo_ready, i)
                for k in range(KD):
                    last = t_.transpose(ps_xT[:, k * P:(k + 1) * P], xg[:, r, k * P:(k + 1) * P], ident[:, :])
                last.then_inc(xT_ps, 1)

            def layer1(i, b):
                e = pe.value_load(tile_expert[0:1, bass.ds(i, 1)], min_val=0, max_val=E - 1)
                pe.wait_ge(w1_ready, i + 1)
                pe.wait_ge(xlo_ready, i + 1)
                if late(i, 2):
                    pe.wait_ge(hlo_ready, 2 * i - 2)
                for c in range(KH):
                    if c % 4 == 0:
                        t_.matmul(ps_h[b][c // 4], b1_parts[:, bass.ds(e, 1), c // 4, :].rearrange("p o m -> p (o m)"),
                                  chunk_of[:, :, :], start=True, stop=False)
                    o = ps_h[b][c // 4][:, (c % 4) * P:(c % 4 + 1) * P]
                    for k in range(KD):
                        for wp, xp in ((0, 0), (0, 1), (1, 0)):
                            w = k * 2 * CH + wp * CH + c * P
                            last = t_.matmul(o, w1s[:, b, w:w + P], xs[:, b, xp, k * P:(k + 1) * P],
                                             start=False, stop=(c % 4 == 3 and k == KD - 1 and wp == 1))
                    if c % 4 == 3:
                        last.then_inc(h_ps, 1)

            def layer2(i, b):
                e = pe.value_load(tile_expert[0:1, bass.ds(i, 1)], min_val=0, max_val=E - 1)
                pe.wait_ge(w2_ready, i + 1)
                pe.wait_ge(hlo_ready, 2 * i + 2)
                if late(i, 2):
                    pe.wait_ge(y_ready, i - 1)
                for c in range(KH):
                    chunk = CPL + c * D // CH
                    low = wsp[:, bass.ds(e * (CPE * 2 * CH) + chunk * 2 * CH + CH + c * D % CH, D)]
                    high = w2s[:, b, c * D:(c + 1) * D]
                    for hp, w in ((0, high), (1, high), (0, low)):
                        last = t_.matmul(ps_y[b], hT[:, b, hp, c * P:(c + 1) * P], w,
                                         start=(c == 0 and w is high and hp == 0), stop=(c == KH - 1 and w is low))
                last.then_inc(y_ps, 1)

            turn_x(0, 0, 0, 1)

            used = load_used(pe)

            def tile(i, b, r, turn, plan=None):
                if_used(pe, used, i + 1, lambda: turn_x(i + 1, 1 - b, (r + 1) % RING, turn + (1 if r == RING - 1 else 0)))
                if_used(pe, used, i, lambda: layer1(i, b))
                if late(i, 1):
                    if_used(pe, used, i - 1, lambda: layer2(i - 1, 1 - b))

            slot_tiles(pe, tile, plans=False)
            i = SLOT_TILES - 1
            if_used(pe, used, i, lambda: layer2(i, i % 2))


def kernel(x, cond_8, L0_cond_weight, L0_cond_mask, L0_cond_bias, L0_ffn_gate_w, L0_ffn_gate_b,
           L0_ffn_w1, L0_ffn_b1, L0_ffn_w2, L0_ffn_b2):
    import numpy as np
    import concourse.bacc as bacc
    from concourse.bass_utils import run_bass_kernel_spmd

    def c(a):
        return np.ascontiguousarray(a)

    x, y, cw, cm, cb, gw, gb, w1, b1, w2, b2 = map(np.asarray, (
        x, cond_8, L0_cond_weight, L0_cond_mask, L0_cond_bias, L0_ffn_gate_w, L0_ffn_gate_b,
        L0_ffn_w1, L0_ffn_b1, L0_ffn_w2, L0_ffn_b2))
    rows = x.reshape(TOK, D)
    w1_l = w1.transpose(0, 2, 1).reshape(E, KD, P, H).transpose(0, 2, 1, 3).reshape(E, P, D * H // P)
    w2_l = w2.transpose(0, 2, 1).reshape(E, KH, P, D).transpose(0, 2, 1, 3).reshape(E, P, D * H // P)
    arrays = {
        "x_t": c(rows.T.reshape(KD, P, TOK).transpose(1, 0, 2)),
        "x_rows": c(rows),
        "cond_y": c(y.reshape(B * G)),
        "cond_w": c(cw.reshape(4, 2, KD, P, D).transpose(0, 3, 1, 2, 4).reshape(4, P, 2, CW)),
        "cond_mask": c(cm.reshape(KD, P, D).transpose(1, 0, 2).reshape(P, CW)),
        "cond_bias": c(cb),
        "gate_t": c(gw.T.reshape(KD, P, E).transpose(1, 0, 2)),
        "gate_b": c(gb),
        "w_all": c(np.concatenate([w1_l, w2_l], axis=2)),
        "b1": c(b1.reshape(E * KH, P)),
        "b2": c(b2),
    }
    nc = bacc.Bacc("TRN2", target_bir_lowering=False, num_devices=1)
    args = [nc.dram_tensor(n, a.shape, mybir.dt.from_np(a.dtype), kind="ExternalInput").ap() for n, a in arrays.items()]
    out = nc.dram_tensor("out", (TOK, D), F32, kind="ExternalOutput").ap()
    build(nc, *args, out)
    r = run_bass_kernel_spmd(nc, [arrays], core_ids=[0])
    return r.results[0]["out"].reshape(B, S, D)
```

```python
from contextlib import ExitStack

import concourse.bass as bass
from concourse import mybir

ALU = mybir.AluOpType
ACT = mybir.ActivationFunctionType
AX = mybir.AxisListType
F32 = mybir.dt.float32
F16 = mybir.dt.float16
BF16 = mybir.dt.bfloat16
I32 = mybir.dt.int32

P = 128
B, S, D = 2, 1024, 256
E, H, G = 8, 1024, 8
TOK = B * S
TT = TOK // P
TPB = S // P
KD = D // P
KH = H // P
SLOT_TILES = TOK // P + E - 1
ST = SLOT_TILES + 1
NT = SLOT_TILES + 3
CW = KD * D
CH = 1024
CPL = D * H // P // CH
CPE = 2 * CPL
CHUNKS = E * CPE
AHEAD = 4
POOL_SPLITS = 3
LOADED = 2 * CPE
EARLY = 7
PER_TILE = 2
WSCALE = 64.0
RING = 4
HALF = KH * P // 2
SURE = TOK // P
LOOPS = (SURE - 2) // RING
AFTER = 2 + LOOPS * RING
STORES = ((0, 6), (6, 11), (11, 14), (14, 16))
B1_ROWS = 36
assert POOL_SPLITS == EARLY - AHEAD
X16_PLACE = LOADED + AHEAD
B1_PLACE = X16_PLACE + 4
EP = 32
CG = P // EP
FIRST_STORES = 2
XC = S // CG


def build(nc, x_t, x_rows, cond_y, cond_w, cond_mask, cond_bias, gate_t, gate_b, w_all, b1, b2, out):
    xf_rows = nc.dram_tensor("xf_rows", [TOK, D], F32, kind="Internal").ap()
    b1_scratch = nc.dram_tensor("b1_scratch", [2, E * KH, P], F16, kind="Internal").ap()
    with ExitStack() as ctx:
        def sb(name, shape, dt=F32):
            return ctx.enter_context(nc.sbuf_tensor(name, shape, dt))

        def sem(name):
            return ctx.enter_context(nc.semaphore(name))

        wsp = sb("wsp", [P, (CHUNKS + AHEAD) * 2 * CH], F16)

        def place32(n):
            return wsp[:, bass.ds(n * 2 * CH, 2 * CH)].bitcast(F32)

        def hi_of(n):
            return wsp[:, bass.ds(n * 2 * CH, CH)]

        def lo_of(n):
            return wsp[:, bass.ds(n * 2 * CH + CH, CH)]

        at = (CHUNKS + AHEAD - 2 * CPE) * 2 * CH
        condw = wsp[:, at:at + CPE * 2 * CH].bitcast(F32).rearrange("p (g n) -> p g n", g=G)
        at += CPE * 2 * CH
        xT = wsp[:, at:at + CPE * 2 * CH].bitcast(F32).rearrange("p (k n) -> p k n", k=KD)

        x16 = wsp[:, X16_PLACE * 2 * CH:(X16_PLACE + 4) * 2 * CH].rearrange("p (a k n) -> p a k n", a=2, k=KD)

        stage = sb("stage", [P, TT * D + 5 * CW])
        xf = stage[:, 0:TT * D].rearrange("p (t n) -> p t n", n=D)
        at = TT * D
        wbot = stage[:, at:at + 2 * CW].rearrange("p (b k n) -> p b k n", b=B, k=KD)
        oh_slot = stage[:, at:at + TT * P // 2].bitcast(BF16).rearrange("p (t n) -> p t n", t=TT)
        at += 2 * CW
        w_t = stage[:, at:at + 2 * CW].bitcast(F16).rearrange("p (b a n) -> p b a n", b=B, a=2)
        at += 2 * CW
        mask = stage[:, at:at + CW]
        w1s = stage[:, 0:2 * CPL * CH].bitcast(F16).rearrange("p (b n) -> p b n", b=2)
        w2s = stage[:, 2 * CPL * CH:3 * CPL * CH].bitcast(F16).rearrange("p (b n) -> p b n", b=2)

        hT = sb("hT", [P, 2, 2, KH * P], F16)
        products = hT[:, :, :, :].rearrange("p b a n -> p (b a n)").bitcast(F32).rearrange("p (r n) -> p r n", n=CW)
        tables = hT[:, :, :, :].rearrange("p b a n -> p (b a n)").bitcast(F32)
        taken = [0]

        def table(words):
            taken[0] += words
            assert taken[0] <= 2 * KH * P
            return tables[:, taken[0] - words:taken[0]]

        logits_t = table(B * XC)
        pick = table(TT * E).rearrange("p (t e) -> p t e", e=E)
        per_tile = table(E * TT)
        upto = table(E * TT).rearrange("p (e t) -> p e t", e=E)
        place = table(E * TT).rearrange("p (e t) -> p e t", e=E)
        sel = table(TT * ST).rearrange("p (t n) -> p t n", n=ST)
        tok_rhs = table(TT * ST).bitcast(BF16).rearrange("p (t n) -> p t n", n=2 * ST)
        past = table(NT * E).rearrange("p (t e) -> p t e", e=E)

        b2_all = sb("b2_all", [P, E, D])
        y_all = sb("y_all", [P, B * G])
        gate = sb("gate", [P, KD, CG * EP])
        bias_col = sb("bias_col", [P, KD])
        gate_w = sb("gate_w", [P, B, KD * EP])
        logit_bias = sb("logit_bias", [P, 1])
        gate_bias = sb("gate_bias", [P, 1])
        b1_parts = sb("b1_parts", [B1_ROWS, E, 2, P], F16)
        chunk_of = sb("chunk_of", [B1_ROWS, 4, P], F16)
        b1_raw = place32(B1_PLACE)[0:E * KH, 0:P]
        b1_split = lo_of(B1_PLACE)[0:E * KH, 0:2 * P].rearrange("p (a m) -> p a m", a=2)
        ident = sb("ident", [P, P])
        ones = sb("ones", [P, E * TT])
        before = sb("before", [P, P], BF16)
        ones_h = sb("ones_h", [P, P], BF16)
        iota_r = sb("iota_r", [P, P], BF16)
        e_less_8 = sb("e_less_8", [P, E])
        tile_no = sb("tile_no", [P, ST])
        tile_at = sb("tile_at", [P, NT])
        usual_goal = sb("usual_goal", [P, NT])
        tok_tile = sb("tok_tile", [P, TT])
        part_no = sb("part_no", [P, 1])

        best = sb("best", [P, TT])
        first = sb("first", [P, TT])
        oh = sb("oh", [P, E, TT], BF16)
        count = sb("count", [P, E])
        padded_i = sb("padded_i", [P, 2, E], I32)
        padded = sb("padded", [P, E])
        ends = sb("ends", [P, E])
        offs = sb("offs", [P, 3, E])
        slot_f = sb("slot_f", [P, TT])
        slot_i = sb("slot_i", [P, 3, TT], I32)
        slot_lo = sb("slot_lo", [P, TT])
        slot_hi = sb("slot_hi", [P, TT])
        tok_f = sb("tok_f", [P, 2 * ST])
        tok_sum = sb("tok_sum", [P, ST])
        tok_of_slot = sb("tok_of_slot", [P, ST], I32)
        tile_e = sb("tile_e", [P, NT])
        goal_f = sb("goal_f", [P, 2, NT])
        same = sb("same", [P, NT])
        packed = sb("packed", [P, 4, ST])
        tile_expert = sb("tile_expert", [P, ST], I32)
        tile_plan = sb("tile_plan", [P, ST], I32)
        tiles_used = sb("tiles_used", [P, 2], I32)

        xg = sb("xg", [P, RING, D])
        res = sb("res", [P, RING, D])
        xs = sb("xs", [P, 2, 2, D], F16)

        psum = ctx.enter_context(nc.psum_tensor("psum", [P, 8, 512], F32))
        ps_prefix = psum[:, 0, 0:E * TT]
        ps_xT = [psum[:, 7 * n, 0:D] for n in range(2)]
        ps_wT = [psum[:, 1, :], psum[:, 2, :]]
        ps_gate = [psum[:, 3, 0:KD * EP], psum[:, 0, 0:KD * EP]]
        ps_gate_bias = psum[:, 7, 0:1]
        ps_logits_t = [psum[:, 5 + b, 0:XC] for b in range(B)]
        ps_logits = psum[:, 3, 0:TT * EP]
        ps_count, ps_tok = psum[:, 1, 0:E * TT], psum[:, 2, 0:2 * ST]
        ps_rows = [psum[:, 4 + n, 0:D] for n in range(4)]
        ps_h = [[psum[:, 1 + 2 * n + q, :] for q in range(2)] for n in range(2)]
        ps_y = [psum[:, 5 + n, 0:D] for n in range(2)]

        ld_y, ld_mask, ld_small, ld_b1, ld_b2 = map(sem, ["ld_y", "ld_mask", "ld_small", "ld_b1", "ld_b2"])
        ld_cw = [sem(f"ld_cw{n}") for n in range(4)]
        ld_x = [sem(f"ld_x{n}") for n in range(B)]
        ld_chunk = [sem(f"ld_chunk{n}") for n in range(CPE)]
        landed = sem("landed")
        consts = sem("consts")
        pool_step = sem("pool_step")
        product_ready = sem("product_ready")
        cond_sum = sem("cond_sum")
        raw_scaled = sem("raw_scaled")
        wbot0_ready = sem("wbot0_ready")
        wbot1_ready = sem("wbot1_ready")
        wT_ps = sem("wT_ps")
        wT_ready = sem("wT_ready")
        wT_lo_ready = sem("wT_lo_ready")
        x16_hi_ready = sem("x16_hi_ready")
        x16_lo_ready = [sem(f"x16_lo_ready{n}") for n in range(4)]
        b1_ready = sem("b1_ready")
        gate_ps = sem("gate_ps")
        gate_w_ready = sem("gate_w_ready")
        gate_bias_ps = sem("gate_bias_ps")
        logit_bias_ready = sem("logit_bias_ready")
        logits_t_ps = sem("logits_t_ps")
        logits_t_ready = sem("logits_t_ready")
        logits_ps = sem("logits_ps")
        rows_ps = sem("rows_ps")
        rows_ready = sem("rows_ready")
        rows_stored = [sem(f"rows_stored{n}") for n in range(len(STORES))]
        hi_ready = sem("hi_ready")
        lo_pool = sem("lo_pool")
        lo_late = sem("lo_late")
        oh_ready = sem("oh_ready")
        rank_ps = sem("rank_ps")
        dve_step = sem("dve_step")
        tok_rhs_ready = sem("tok_rhs_ready")
        tok_ps = sem("tok_ps")
        experts_known = sem("experts_known")
        routed = sem("routed")
        x_in = [sem(f"x_in{n}") for n in range(RING)]
        res_in = [sem(f"res_in{n}") for n in range(RING)]
        stored = [sem(f"stored{n}") for n in range(RING)]
        res_ready = sem("res_ready")
        xT_ps = sem("xT_ps")
        xhi_ready = sem("xhi_ready")
        xlo_ready = sem("xlo_ready")
        w1_ready = sem("w1_ready")
        w2_ready = sem("w2_ready")
        h_ps = sem("h_ps")
        b1_high = sem("b1_high")
        b1_low = sem("b1_low")
        b1_stored = sem("b1_stored")
        hhi_ready = sem("hhi_ready")
        hlo_ready = sem("hlo_ready")
        y_ps = sem("y_ps")
        y_ready = sem("y_ready")

        N_CONST = 12
        RANKS_AFTER = 3
        HIGH_AFTER = (7, 12)

        def quarter(q):
            return slice(q * TOK // 4, (q + 1) * TOK // 4)

        def late(i, n):
            return not isinstance(i, int) or i >= n

        class Plan:
            def __init__(self, eng, i):
                word = eng.value_load(tile_plan[0:1, bass.ds(i + 1, 1)], min_val=0, max_val=(1 << 18) - 1)
                self.expert, self.next_expert = word & 7, (word >> 3) & 7
                self.goal, self.next_goal = (word >> 6) & 31, (word >> 11) & 31
                self.same, self.next_same = (word >> 16) & 1, (word >> 17) & 1

        def following_plan(eng, i, plan):
            return None if isinstance(i, int) and i == SLOT_TILES - 1 else Plan(eng, i + 1)

        def split_chunks(eng, split, done, goal):
            more = goal - done
            with eng.If(more > 0):
                with eng.Fori(0, more) as m:
                    split(nc.s_assert_within(done + m, 0, CHUNKS - EARLY - 1, skip_runtime_bounds_check_because=
                                             "done + m < goal, which is at most CHUNKS - EARLY"))
            with eng.Else():
                eng.nop()

        def if_used(eng, used, i, work):
            if not isinstance(i, int) or i < SURE:
                work()
            elif i < SLOT_TILES:
                with eng.If(used > i):
                    work()
                with eng.Else():
                    eng.nop()

        def load_used(eng):
            return eng.value_load(tiles_used[0:1, 1:2], min_val=SURE, max_val=SLOT_TILES)

        def slot_tiles(eng, tile, plans=True):
            plan = tile(0, 0, 0, 1, plans and Plan(eng, 0))
            tile(1, 1, 1, 1, plan)
            with eng.Fori(0, LOOPS) as j:
                plan = plans and Plan(eng, RING * j + 2)
                for u in range(RING):
                    plan = tile(RING * j + 2 + u, u % 2, (2 + u) % RING, j + 1 + (2 + u) // RING, plan)
            plan = plans and Plan(eng, AFTER)
            for i in range(AFTER, SLOT_TILES):
                plan = tile(i, i % 2, i % RING, i // RING + 1, plan)

        block = ctx.enter_context(nc.Block())

        @block.sync
        def _(sp):
            sp.dma_start(y_all[:, :], cond_y.partition_broadcast(P)).then_inc(ld_y, 16)
            for n in range(4):
                sp.dma_start(condw[:, 2 * n:2 * n + 2, :], cond_w[n]).then_inc(ld_cw[n], 16)
                if n == 0:
                    sp.dma_start(mask, cond_mask).then_inc(ld_mask, 16)

            for b in range(B):
                sp.dma_start(xT[:, :, b * S:(b + 1) * S], x_t[:, :, b * S:(b + 1) * S]).then_inc(ld_x[b], 16)

            def load_chunk(e, q):
                src = w_all[bass.ds(e, 1), :, q * CH:(q + 1) * CH].rearrange("o p n -> (o p) n")
                sp.dma_start(place32(e * CPE + q + AHEAD), src).then_inc(ld_chunk[q], 16)

            def confirm(q, turn):
                sp.wait_ge(ld_chunk[q], 16 * turn)
                sp.sem_inc(landed, 1)

            def store_rows(n):
                t, end = STORES[n]
                sp.wait_ge(rows_ready, end)
                sp.dma_start(xf_rows[t * P:end * P, :].rearrange("(t p) d -> p t d", p=P),
                             xf[:, t:end, :]).then_inc(rows_stored[n], 16)

            for q in range(CPE):
                load_chunk(0, q)
            for e in range(1, LOADED // CPE):
                for q in range(CPE):
                    confirm(q, e)
                    load_chunk(e, q)
            sp.wait_ge(b1_low, 1)
            sp.dma_start(b1_scratch.rearrange("a r m -> r a m"), b1_split[:, :, :]).then_inc(b1_stored, 16)
            for n in range(len(STORES)):
                store_rows(n)
            for q in range(CPE):
                confirm(q, LOADED // CPE)
            sp.wait_ge(consts, N_CONST)
            sp.wait_ge(b1_stored, 16)
            for part in range(2):
                sp.dma_start(b1_parts[32 * part:32 * part + 4, :, :, :],
                             b1_scratch[part].rearrange("(e q c) m -> c e q m", e=E, q=2)).then_inc(b1_ready, 16)
            sp.wait_ge(x_in[1], 16)
            sp.wait_ge(wbot0_ready, 1)
            sp.wait_ge(wbot1_ready, 1)
            sp.wait_ge(rows_ps, TT)
            sp.wait_ge(b1_ready, 32)
            for n in range(len(STORES)):
                sp.wait_ge(rows_stored[n], 16)
            load_chunk(LOADED // CPE, 0)
            load_chunk(LOADED // CPE, 1)
            sp.dma_start(b2_all[:, :, :], b2.partition_broadcast(P)).then_inc(ld_b2, 16)
            with sp.Fori(LOADED // CPE, E - 1) as e:
                for q in range(CPE):
                    confirm(q, e + 1)
                    load_chunk(e + (q + 2) // CPE, (q + 2) % CPE)
            for q in range(CPE):
                confirm(q, E)
                if q + 2 < CPE:
                    load_chunk(E - 1, q + 2)

        @block.gpsimd
        def _(pool):
            g = nc.gpsimd
            g.memset(ident[:, :], 0.0).then_inc(pool_step, 1)
            g.memset(ones_h[:, :], 1.0).then_inc(pool_step, 1)
            pool.wait_ge(pool_step, 2)
            g.affine_select(out=ident[:, :], in_=ident[:, :], compare_op=ALU.not_equal, fill=1.0, base=0,
                            pattern=[[-1, P]], channel_multiplier=1).then_inc(consts, 1)
            g.memset(ones[:, :], 1.0).then_inc(consts, 1)
            g.memset(b1_parts[:, :, :, :], 0.0).then_inc(consts, 1)
            g.memset(chunk_of[:, :, :], 0.0).then_inc(pool_step, 1)
            for n, row in enumerate((0, 32)):
                pool.wait_ge(pool_step, n + 3)
                g.affine_select(out=chunk_of[row:row + 4, :, :], in_=chunk_of[row:row + 4, :, :],
                                compare_op=ALU.not_equal, fill=1.0, base=0, pattern=[[-1, 4], [0, P]],
                                channel_multiplier=1).then_inc(pool_step, 1)
            pool.wait_ge(pool_step, 5)
            acc = wbot[:, 1, :, :].rearrange("p k n -> p (k n)")
            for n in range(1, 4):
                pool.wait_ge(product_ready, n + 1)
                g.tensor_tensor(acc, products[:, 0, :] if n == 1 else acc, products[:, n, :], ALU.add).then_inc(cond_sum, 1)
                pool.wait_ge(cond_sum, n)
            g.affine_select(out=before[:, :], in_=ones_h[:, :], compare_op=ALU.is_gt, fill=0.0, base=0,
                            pattern=[[1, P]], channel_multiplier=-1).then_inc(consts, 1)

            def iota(t, pattern, base=0, cm=0):
                g.iota(t, pattern, base=base, channel_multiplier=cm,
                       allow_small_or_imprecise_dtypes=True).then_inc(consts, 1)

            iota(iota_r[:, :], [[1, P]])
            iota(e_less_8[:, :], [[1, E]], base=-E)
            iota(tile_no[:, :], [[1, ST]])
            iota(tile_at[:, :], [[P, NT]], base=-P)
            iota(tok_tile[:, :], [[1, TT]], base=-TT)
            iota(part_no[:, :], [[0, 1]], cm=1)
            iota(usual_goal[:, :], [[PER_TILE, NT]], base=-2 * PER_TILE)
            g.memset(same[:, :], 0.0).then_inc(consts, 1)
            g.memset(xg[:, :, :], 0.0).then_inc(pool_step, 1)
            g.memset(res[:, :, :], 0.0).then_inc(pool_step, 1)

            for q in (0, 1, 3):
                pool.wait_ge(x16_hi_ready, q + 1)
                part = quarter(q)
                g.tensor_tensor(x16[:, 1, :, part], xT[:, :, part], x16[:, 0, :, part],
                                ALU.subtract).then_inc(x16_lo_ready[q], 1)
            for n in range(POOL_SPLITS):
                pool.wait_ge(hi_ready, n + 1)
                raw = place32(n + AHEAD)
                g.tensor_scalar(raw, raw, WSCALE, 1.0, ALU.mult, ALU.mult).then_inc(raw_scaled, 1)
                pool.wait_ge(raw_scaled, n + 1)
                g.tensor_tensor(lo_of(n), raw, hi_of(n), ALU.subtract).then_inc(lo_pool, 1)

            def token(i):
                return bass.IndirectOffsetOnAxis(ap=tok_of_slot[:, i:i + 1], axis=0)

            def gather_x(i):
                if i >= RING:
                    pool.wait_ge(xT_ps, i - RING + 1)
                g.indirect_dma_start(xg[:, i % RING, :], None, xf_rows, token(i),
                                     bounds_check=TOK - 1, oob_is_err=False).then_inc(x_in[i % RING], 16)

            def gather_res(i):
                if i >= RING:
                    pool.wait_ge(stored[i % RING], 16 * (i // RING))
                g.indirect_dma_start(res[:, i % RING, :], None, x_rows, token(i),
                                     bounds_check=TOK - 1, oob_is_err=False).then_inc(res_in[i % RING], 16)

            def add_b2(i):
                e = pool.value_load(tile_expert[0:1, i:i + 1], min_val=0, max_val=E - 1)
                pool.wait_ge(res_in[i % RING], 16 * (i // RING + 1))
                g.tensor_tensor(res[:, i % RING, :], res[:, i % RING, :],
                                b2_all[:, bass.ds(e, 1), :].rearrange("p a n -> p (a n)"), ALU.add).then_inc(res_ready, 1)

            def scatter(i):
                pool.wait_ge(y_ready, i + 1)
                g.indirect_dma_start(out, token(i), res[:, i % RING, :], None,
                                     bounds_check=TOK - 1, oob_is_err=False).then_inc(stored[i % RING], 16)

            pool.wait_ge(pool_step, 7)
            for n in range(len(STORES)):
                pool.wait_ge(rows_stored[n], 16)
            pool.wait_ge(routed, 1)
            for i in range(RING):
                gather_x(i)
            gather_res(0)
            pool.wait_ge(ld_b2, 16)
            pool.wait_ge(experts_known, 1)
            used = load_used(pool)
            for i in range(SLOT_TILES + 2):
                if_used(pool, used, i + RING, lambda: gather_x(i + RING))
                if_used(pool, used, i + 1, lambda: gather_res(i + 1))
                if_used(pool, used, i, lambda: add_b2(i))
                if i >= 2:
                    if_used(pool, used, i - 2, lambda: scatter(i - 2))
            for i in range(SURE - RING, SLOT_TILES):
                if_used(pool, used, i, lambda: pool.wait_ge(stored[i % RING], 16 * (i // RING + 1)))

        @block.scalar
        def _(act):
            a = nc.scalar
            act.dma_start(gate[:, :, :], gate_t).then_inc(ld_small, 16)
            act.dma_start(bias_col[:, :], cond_bias.rearrange("(k p) -> p k", p=P),
                          allow_slow_non_contiguous=True).then_inc(ld_small, 16)
            act.dma_start(b1_raw[:, :], b1).then_inc(ld_b1, 16)
            act.dma_start(gate_bias[:, :], gate_b).then_inc(ld_small, 16)
            act.wait_ge(ld_b1, 16)
            a.mul(b1_split[:, 0, :], b1_raw[:, :], WSCALE).then_inc(b1_high, 1)
            act.wait_ge(ld_y, 16)
            for n in range(4):
                if n % 2 == 0:
                    act.wait_ge(ld_cw[n // 2], 16)
                a.mul(products[:, n, :], condw[:, n, :], y_all[:, G + n:G + n + 1]).then_inc(product_ready, 1)

            def x_high(q):
                act.wait_ge(ld_x[q // 2], 16)
                part = quarter(q)
                a.copy(x16[:, 0, :, part], xT[:, :, part]).then_inc(x16_hi_ready, 1)

            def w_t_out(b):
                act.wait_ge(wT_ps, b + 1)
                a.mul(w_t[:, b, 0, :], ps_wT[b], WSCALE).then_inc(wT_ready, 1)

            def high(n):
                act.wait_ge(landed, n + 1)
                if n >= AHEAD:
                    act.wait_ge(lo_pool, n - AHEAD + 1)
                a.mul(hi_of(n), place32(n + AHEAD), WSCALE).then_inc(hi_ready, 1)

            act.wait_ge(gate_ps, 1)
            a.copy(gate_w[:, 0, :], ps_gate[0]).then_inc(gate_w_ready, 1)
            act.wait_ge(ld_small, 48)
            act.wait_ge(gate_bias_ps, 1)
            a.activation(logit_bias[:, :], ps_gate_bias, ACT.Identity, bias=gate_bias[:, 0:1]).then_inc(logit_bias_ready, 1)
            x_high(0)
            x_high(1)
            w_t_out(0)
            x_high(2)
            x_high(3)
            w_t_out(1)
            high(0)
            high(1)

            for t in range(TT):
                act.wait_ge(rows_ps, t + 1)
                a.mul(xf[:, t, :], ps_rows[t % 4], 1.0 / WSCALE).then_inc(rows_ready, 1)
                if t in HIGH_AFTER:
                    high(B + HIGH_AFTER.index(t))

            def high_late(m):
                act.wait_ge(landed, m + EARLY + 1)
                act.wait_ge(lo_late, m + 1)
                a.mul(hi_of(m + EARLY), place32(m + EARLY + AHEAD), WSCALE).then_inc(hi_ready, 1)

            for n in range(B + len(HIGH_AFTER), EARLY):
                high(n)
            act.wait_ge(experts_known, 1)

            def w2_copy(i, b, plan):
                act.wait_ge(hi_ready, plan.goal + EARLY)
                if late(i, 2):
                    act.wait_ge(y_ps, i - 1)
                src = wsp[:, bass.ds(plan.expert * (CPE * 2 * CH) + CPL * 2 * CH, CPL * 2 * CH)].rearrange(
                    "p (c a n) -> p c a n", c=CPL, a=2)[:, :, 0, :]

                def copy():
                    a.copy(w2s[:, b, :].rearrange("p (c n) -> p c n", c=CPL), src).then_inc(w2_ready, 1)

                if late(i, 2):
                    with act.If(plan.same == 0):
                        copy()
                    with act.Else():
                        act.wait_ge(w2_ready, i)
                        act.nop().then_inc(w2_ready, 1)
                else:
                    copy()

            def x_hi(i, b):
                act.wait_ge(xT_ps, i + 1)
                if late(i, 2):
                    act.wait_ge(h_ps, 2 * i - 2)
                for k in range(KD):
                    last = a.activation(xs[:, b, 0, k * P:(k + 1) * P], ps_xT[b][:, k * P:(k + 1) * P], ACT.Identity,
                                        bias=bias_col[:, k:k + 1])
                last.then_inc(xhi_ready, 1)

            def h_hi(i, b):
                if late(i, 2):
                    act.wait_ge(y_ps, i - 1)
                for q in range(2):
                    act.wait_ge(h_ps, 2 * i + q + 1)
                    a.activation(hT[:, b, 0, q * HALF:(q + 1) * HALF], ps_h[b][q], ACT.Relu).then_inc(hhi_ready, 1)

            used = load_used(act)
            plan = Plan(act, -1)
            split_chunks(act, high_late, 0, plan.goal)
            x_hi(0, 0)
            split_chunks(act, high_late, plan.goal, plan.next_goal)

            def tile(i, b, r, turn, plan):
                if_used(act, used, i + 1, lambda: x_hi(i + 1, 1 - b))
                if_used(act, used, i + 2, lambda: split_chunks(act, high_late, plan.goal, plan.next_goal))
                next_plan = following_plan(act, i, plan)
                if_used(act, used, i, lambda: w2_copy(i, b, plan))
                if_used(act, used, i, lambda: h_hi(i, b))
                return next_plan

            slot_tiles(act, tile)

        @block.vector
        def _(dve):
            v = nc.vector
            step = [0]

            def then(ins):
                ins.then_inc(dve_step, 1)
                step[0] += 1
                dve.wait_ge(dve_step, step[0])

            dve.wait_ge(ld_y, 16)
            acc = wbot[:, 0, :, :].rearrange("p k n -> p (k n)")
            for n in range(G):
                if n % 2 == 0:
                    dve.wait_ge(ld_cw[n // 2], 16)
                if n == 0:
                    then(v.tensor_scalar(acc, condw[:, 0, :], y_all[:, 0:1], None, ALU.mult))
                else:
                    then(v.scalar_tensor_tensor(acc, condw[:, n, :], y_all[:, n:n + 1], acc, ALU.mult, ALU.add))
            dve.wait_ge(ld_mask, 16)
            v.tensor_tensor(acc, acc, mask, ALU.mult).then_inc(wbot0_ready, 1)
            acc = wbot[:, 1, :, :].rearrange("p k n -> p (k n)")
            dve.wait_ge(cond_sum, 3)
            for n in range(4, G):
                then(v.scalar_tensor_tensor(acc, condw[:, n, :], y_all[:, G + n:G + n + 1], acc, ALU.mult, ALU.add))
            v.tensor_tensor(acc, acc, mask, ALU.mult).then_inc(wbot1_ready, 1)
            def logits_t_out(b):
                dve.wait_ge(logits_t_ps, b + 1)
                v.tensor_scalar(logits_t[:, b * XC:(b + 1) * XC], ps_logits_t[b], logit_bias[:, 0:1], None,
                                ALU.add).then_inc(logits_t_ready, 1)

            def x_low(q):
                dve.wait_ge(x16_hi_ready, q + 1)
                part = quarter(q)
                v.tensor_tensor(x16[:, 1, :, part], xT[:, :, part], x16[:, 0, :, part],
                                ALU.subtract).then_inc(x16_lo_ready[q], 1)

            def w_t_low(b):
                dve.wait_ge(wT_ready, b + 1)
                v.scalar_tensor_tensor(w_t[:, b, 1, :], ps_wT[b], WSCALE, w_t[:, b, 0, :],
                                       ALU.mult, ALU.subtract).then_inc(wT_lo_ready, 1)

            dve.wait_ge(b1_high, 1)
            v.scalar_tensor_tensor(b1_split[:, 1, :], b1_raw[:, :], WSCALE, b1_split[:, 0, :],
                                   ALU.mult, ALU.subtract).then_inc(b1_low, 1)
            dve.wait_ge(logit_bias_ready, 1)
            logits_t_out(0)
            dve.wait_ge(gate_ps, 2)
            v.tensor_copy(gate_w[:, 1, :], ps_gate[1]).then_inc(gate_w_ready, 1)
            w_t_low(0)
            x_low(2)
            logits_t_out(1)
            w_t_low(1)

            def low(n):
                dve.wait_ge(hi_ready, n + 1)
                v.scalar_tensor_tensor(lo_of(n), place32(n + AHEAD), WSCALE, hi_of(n),
                                       ALU.mult, ALU.subtract).then_inc(lo_late, 1)

            def low_late(m):
                dve.wait_ge(hi_ready, m + EARLY + 1)
                v.scalar_tensor_tensor(lo_of(m + EARLY), place32(m + EARLY + AHEAD), WSCALE, hi_of(m + EARLY),
                                       ALU.mult, ALU.subtract).then_inc(lo_late, 1)

            def over_e(t):
                return t.unsqueeze(2).to_broadcast([P, TT, E])

            e_bc = e_less_8[:, :].unsqueeze(1).to_broadcast([P, TT, E])
            dve.wait_ge(logits_ps, 1)
            logits = ps_logits.rearrange("p (t e) -> p t e", e=EP)[:, :, 0:E]
            dve.wait_ge(consts, N_CONST)
            then(v.tensor_reduce(best[:, :], logits, AX.X, ALU.max))
            then(v.tensor_tensor(pick[:, :, :], logits, over_e(best[:, :]), ALU.is_equal))
            then(v.tensor_tensor(pick[:, :, :], pick[:, :, :], e_bc, ALU.mult))
            then(v.tensor_reduce(first[:, :], pick[:, :, :], AX.X, ALU.min))
            v.tensor_tensor(oh[:, :, :].rearrange("p e t -> p t e"), e_bc, over_e(first[:, :]),
                            ALU.is_equal).then_inc(oh_ready, 1)

            dve.wait_ge(rank_ps, 1)
            then(v.tensor_copy(per_tile[:, :], ps_count))
            v.tensor_reduce(count[:, :], per_tile[:, :].rearrange("p (e t) -> p e t", e=E), AX.X, ALU.add)
            upto_f = upto[:, :, :].rearrange("p e t -> p (e t)")
            then(v.tensor_tensor_scan(upto_f, ones[:, 0:E * TT], per_tile[:, :], 0.0, ALU.mult, ALU.add))
            then(v.tensor_scalar(padded_i[:, 0, :], count[:, :], float(P - 1), None, ALU.add))
            then(v.tensor_scalar(padded_i[:, 1, :], padded_i[:, 0, :], -P, None, ALU.bitwise_and))
            then(v.tensor_copy(padded[:, :], padded_i[:, 1, :]))
            v.tensor_tensor(offs[:, 1, :], upto[:, :, TT - 1], count[:, :], ALU.subtract)
            then(v.tensor_tensor_scan(ends[:, :], ones[:, 0:E], padded[:, :], 0.0, ALU.mult, ALU.add))
            then(v.tensor_tensor(offs[:, 0, :], ends[:, :], padded[:, :], ALU.subtract))
            then(v.tensor_tensor(offs[:, 2, :], offs[:, 0, :], offs[:, 1, :], ALU.subtract))
            place_f = place[:, :, :].rearrange("p e t -> p (e t)")
            then(v.tensor_tensor(place_f, upto_f, per_tile[:, :], ALU.subtract))
            then(v.tensor_tensor(place_f, ps_prefix, place_f, ALU.add))
            then(v.tensor_tensor(place[:, :, :], place[:, :, :], offs[:, 2, :].unsqueeze(2).to_broadcast([P, E, TT]), ALU.add))
            then(v.tensor_tensor(place[:, :, :], place[:, :, :], oh[:, :, :], ALU.mult))
            then(v.tensor_reduce(slot_f[:, :], place[:, :, :].rearrange("p e t -> p t e"), AX.X, ALU.add))
            then(v.tensor_copy(slot_i[:, 0, :], slot_f[:, :]))
            v.tensor_scalar(slot_i[:, 1, :], slot_i[:, 0, :], P - 1, None, ALU.bitwise_and)
            then(v.tensor_scalar(slot_i[:, 2, :], slot_i[:, 0, :], 7, None, ALU.logical_shift_right))
            v.tensor_copy(slot_lo[:, :], slot_i[:, 1, :])
            then(v.tensor_copy(slot_hi[:, :], slot_i[:, 2, :]))
            then(v.tensor_tensor(sel[:, :, :], tile_no[:, :].unsqueeze(1).to_broadcast([P, TT, ST]),
                                 slot_hi[:, :].unsqueeze(2).to_broadcast([P, TT, ST]), ALU.is_equal))
            v.tensor_scalar(tok_rhs[:, :, 0:ST], sel[:, :, :], part_no[:, 0:1], None, ALU.mult)
            v.tensor_tensor(tok_rhs[:, :, ST:2 * ST], sel[:, :, :],
                            tok_tile[:, :].unsqueeze(2).to_broadcast([P, TT, ST]), ALU.mult).then_inc(tok_rhs_ready, 1)
            for t in range(TT):
                v.tensor_scalar(oh_slot[:, t, :], iota_r[:, :], slot_lo[:, t:t + 1], None, ALU.is_equal).then_inc(tok_rhs_ready, 1)
            dve.wait_ge(tok_ps, 1)
            then(v.tensor_copy(tok_f[:, :], ps_tok))
            then(v.scalar_tensor_tensor(tok_sum[:, :], tok_f[:, ST:2 * ST], float(P), tok_f[:, 0:ST], ALU.mult, ALU.add))
            v.tensor_scalar(tok_of_slot[:, :], tok_sum[:, :], float(TOK), None, ALU.add).then_inc(routed, 1)
            then(v.tensor_tensor(past[:, :, :], ends[:, :].unsqueeze(1).to_broadcast([P, NT, E]),
                                 tile_at[:, :].unsqueeze(2).to_broadcast([P, NT, E]), ALU.is_le))
            then(v.tensor_reduce(tile_e[:, :], past[:, :, :], AX.X, ALU.add))
            then(v.tensor_scalar(tile_e[:, :], tile_e[:, :], float(E - 1), None, ALU.min))
            v.tensor_copy(tile_expert[:, :], tile_e[:, 1:1 + ST])
            then(v.tensor_scalar(goal_f[:, 0, :], tile_e[:, :], float(CPE), float(CPE - EARLY), ALU.mult, ALU.add))
            then(v.tensor_tensor(goal_f[:, 0, :], goal_f[:, 0, :], usual_goal[:, :], ALU.max))
            then(v.tensor_scalar(goal_f[:, 1, :], goal_f[:, 0, :], float(CHUNKS - EARLY), 0.0, ALU.min, ALU.max))
            v.tensor_tensor(same[:, 2:NT], tile_e[:, 2:NT], tile_e[:, 0:NT - 2], ALU.is_equal)
            then(v.tensor_scalar(tiles_used[:, 0:1], ends[:, E - 1:E], 1.0, None, ALU.mult))
            v.tensor_scalar(tiles_used[:, 1:2], tiles_used[:, 0:1], 7, None, ALU.logical_shift_right)
            v.scalar_tensor_tensor(packed[:, 0, :], tile_e[:, 1:1 + ST], 8.0, tile_e[:, 0:ST], ALU.mult, ALU.add)
            then(v.scalar_tensor_tensor(packed[:, 1, :], goal_f[:, 1, 2:2 + ST], 32.0, goal_f[:, 1, 1:1 + ST], ALU.mult, ALU.add))
            v.scalar_tensor_tensor(packed[:, 2, :], packed[:, 1, :], 64.0, packed[:, 0, :], ALU.mult, ALU.add)
            then(v.scalar_tensor_tensor(packed[:, 3, :], same[:, 1:1 + ST], 2.0, same[:, 0:ST], ALU.mult, ALU.add))
            then(v.scalar_tensor_tensor(tile_plan[:, :], packed[:, 3, :], 65536.0, packed[:, 2, :], ALU.mult, ALU.add))
            v.nop().then_inc(experts_known, 1)
            dve.wait_ge(experts_known, 1)
            dve.wait_ge(lo_pool, POOL_SPLITS)
            dve.wait_ge(tok_ps, 1)

            def w1_into(b, expert):
                v.tensor_copy(w1s[:, b, :], wsp[:, bass.ds(expert * (CPE * 2 * CH), CPL * 2 * CH)]).then_inc(w1_ready, 1)

            def w1_copy(i, b, plan):
                dve.wait_ge(lo_late, plan.goal + AHEAD)
                if late(i, 2):
                    dve.wait_ge(h_ps, 2 * i - 2)
                    with dve.If(plan.next_same == 0):
                        w1_into(b, plan.next_expert)
                    with dve.Else():
                        dve.wait_ge(w1_ready, i)
                        dve.nop().then_inc(w1_ready, 1)
                else:
                    w1_into(b, plan.next_expert)

            def x_lo(i, b):
                dve.wait_ge(xhi_ready, i + 1)
                for k in range(KD):
                    last = v.scalar_tensor_tensor(xs[:, b, 1, k * P:(k + 1) * P], ps_xT[b][:, k * P:(k + 1) * P],
                                                  bias_col[:, k:k + 1], xs[:, b, 0, k * P:(k + 1) * P],
                                                  ALU.add, ALU.subtract)
                last.then_inc(xlo_ready, 1)

            def h_lo(i, b):
                for q in range(2):
                    dve.wait_ge(hhi_ready, 2 * i + q + 1)
                    v.scalar_tensor_tensor(hT[:, b, 1, q * HALF:(q + 1) * HALF], ps_h[b][q], 0.0,
                                           hT[:, b, 0, q * HALF:(q + 1) * HALF], ALU.max, ALU.subtract).then_inc(hlo_ready, 1)

            def y_out(i, b, r):
                dve.wait_ge(y_ps, i + 1)
                dve.wait_ge(res_ready, i + 1)
                v.scalar_tensor_tensor(res[:, r, :], ps_y[b], 1.0 / (WSCALE * WSCALE), res[:, r, :],
                                       ALU.mult, ALU.add).then_inc(y_ready, 1)

            used = load_used(dve)
            plan = Plan(dve, -1)
            for n in range(FIRST_STORES):
                dve.wait_ge(rows_stored[n], 16)
            with dve.If(plan.next_expert == 0):
                w1_into(0, 0)
            with dve.Else():
                dve.nop()
            low(POOL_SPLITS)
            low(POOL_SPLITS + 1)
            x_lo(0, 0)
            for n in range(POOL_SPLITS + 2, EARLY):
                low(n)
            for n in range(FIRST_STORES, len(STORES)):
                dve.wait_ge(rows_stored[n], 16)
            split_chunks(dve, low_late, 0, plan.goal)
            with dve.If(plan.next_expert > 0):
                w1_copy(0, 0, plan)
            with dve.Else():
                dve.nop()
            split_chunks(dve, low_late, plan.goal, plan.next_goal)

            def tile(i, b, r, turn, plan):
                if_used(dve, used, i + 1, lambda: w1_copy(i + 1, 1 - b, plan))
                if_used(dve, used, i + 1, lambda: x_lo(i + 1, 1 - b))
                if late(i, 2):
                    if_used(dve, used, i - 2, lambda: y_out(i - 2, b, (r - 2) % RING))
                if_used(dve, used, i + 2, lambda: split_chunks(dve, low_late, plan.goal, plan.next_goal))
                next_plan = following_plan(dve, i, plan)
                if_used(dve, used, i, lambda: h_lo(i, b))
                return next_plan

            slot_tiles(dve, tile)
            for i in (SLOT_TILES - 2, SLOT_TILES - 1):
                if_used(dve, used, i, lambda: y_out(i, i % 2, i % RING))

        @block.tensor
        def _(pe):
            t_ = nc.tensor

            def turn_w(b):
                pe.wait_ge([wbot0_ready, wbot1_ready][b], 1)
                for kt in range(KD):
                    for ko in range(KD):
                        last = t_.transpose(ps_wT[b][:, kt * D + ko * P:kt * D + ko * P + P],
                                            wbot[:, b, ko, kt * P:kt * P + P], ident[:, :])
                last.then_inc(wT_ps, 1)

            def fold_gate(b):
                for kt in range(KD):
                    for ko in range(KD):
                        last = t_.matmul(ps_gate[b][:, kt * EP:(kt + 1) * EP], wbot[:, b, ko, kt * P:kt * P + P],
                                         gate[:, ko, 0:EP], start=(ko == 0), stop=(ko == KD - 1))
                last.then_inc(gate_ps, 1)

            def rows(t):
                b = t // TPB
                if t % TPB == 0:
                    pe.wait_ge(wT_ready, b + 1)
                    pe.wait_ge(wT_lo_ready, b + 1)
                if t % (TT // 4) == 0:
                    pe.wait_ge(x16_lo_ready[t // (TT // 4)], 1)
                if t >= 4:
                    pe.wait_ge(rows_ready, t - 3)
                for k in range(KD):
                    for xp, wp in ((0, 0), (0, 1), (1, 0)):
                        last = t_.matmul(ps_rows[t % 4], x16[:, xp, k, t * P:(t + 1) * P],
                                         w_t[:, b, wp, k * D:(k + 1) * D], start=(k + xp + wp == 0),
                                         stop=(k == KD - 1 and xp == 1))
                last.then_inc(rows_ps, 1)

            def gate_logits(b):
                pe.wait_ge(ld_x[b], 16)
                pe.wait_ge(gate_w_ready, b + 1)
                tokens = xT[:, :, b * S:(b + 1) * S].rearrange("p k (h j n) -> p k j h n", j=CG, n=P)
                for k in range(KD):
                    for j in range(CG):
                        last = t_.matmul(ps_logits_t[b][j * EP:(j + 1) * EP, :], gate_w[:, b, k * EP:(k + 1) * EP],
                                         tokens[:, k, j, :, :], start=(k == 0), stop=(k == KD - 1))
                last.then_inc(logits_t_ps, 1)

            def turn_logits(b):
                pe.wait_ge(logits_t_ready, b + 1)
                for h in range(XC // P):
                    n = b * XC + h * P
                    last = t_.transpose(ps_logits[:, n:n + P], logits_t[:, n:n + P], ident[:, :])
                return last

            def keep_clock_up(n):
                for _ in range(n):
                    t_.matmul(psum[:, 6, :], ones_h[:, :], ones_h[:, :].unsqueeze(1).to_broadcast([P, 4, P]),
                              start=True, stop=True)

            pe.wait_ge(consts, 2)
            pe.wait_ge(ld_cw[2], 16)
            keep_clock_up(10)
            pe.wait_ge(ld_small, 48)
            pe.wait_ge(wbot0_ready, 1)
            fold_gate(0)
            turn_w(0)
            for ko in range(KD):
                last = t_.matmul(ps_gate_bias, gate[:, ko, :], bias_col[:, ko:ko + 1], start=(ko == 0), stop=(ko == KD - 1))
            last.then_inc(gate_bias_ps, 1)
            gate_logits(0)
            pe.wait_ge(wbot1_ready, 1)
            fold_gate(1)
            turn_w(1)
            pe.wait_ge(logit_bias_ready, 1)
            gate_logits(1)
            turn_logits(0)
            turn_logits(1).then_inc(logits_ps, 1)
            for t in range(RANKS_AFTER):
                rows(t)
            pe.wait_ge(oh_ready, 1)
            pe.wait_ge(consts, N_CONST)
            oh_f = oh[:, :, :].rearrange("p e t -> p (e t)")
            t_.matmul(ps_prefix, before[:, :], oh_f, start=True, stop=True)
            t_.matmul(ps_count, ones_h[:, :], oh_f, start=True, stop=True).then_inc(rank_ps, 1)
            for t in range(RANKS_AFTER, TT):
                rows(t)
            for t in range(TT):
                pe.wait_ge(tok_rhs_ready, t + 2)
                last = t_.matmul(ps_tok, oh_slot[:, t, :], tok_rhs[:, t, :], start=(t == 0), stop=(t == TT - 1))
            last.then_inc(tok_ps, 1)

            pe.wait_ge(routed, 1)
            pe.wait_ge(rows_ready, TT)
            keep_clock_up(26)
            pe.wait_ge(experts_known, 1)
            pe.wait_ge(b1_ready, 32)


            def turn_x(i, b, r, turn):
                pe.wait_ge(x_in[r], 16 * turn)
                if late(i, 2):
                    pe.wait_ge(xlo_ready, i - 1)
                for k in range(KD):
                    last = t_.transpose(ps_xT[b][:, k * P:(k + 1) * P], xg[:, r, k * P:(k + 1) * P], ident[:, :])
                last.then_inc(xT_ps, 1)

            def layer1(i, b, e):
                pe.wait_ge(w1_ready, i + 1)
                pe.wait_ge(xlo_ready, i + 1)
                if late(i, 2):
                    pe.wait_ge(hlo_ready, 2 * i - 2)
                for c in range(KH):
                    if c % 4 == 0:
                        t_.matmul(ps_h[b][c // 4], b1_parts[:, bass.ds(e, 1), c // 4, :].rearrange("p o m -> p (o m)"),
                                  chunk_of[:, :, :], start=True, stop=False)
                    o = ps_h[b][c // 4][:, (c % 4) * P:(c % 4 + 1) * P]
                    for k in range(KD):
                        for wp, xp in ((0, 0), (0, 1), (1, 0)):
                            w = k * 2 * CH + wp * CH + c * P
                            last = t_.matmul(o, w1s[:, b, w:w + P], xs[:, b, xp, k * P:(k + 1) * P],
                                             start=False, stop=(c % 4 == 3 and k == KD - 1 and wp == 1))
                    if c % 4 == 3:
                        last.then_inc(h_ps, 1)

            def layer2(i, b):
                e = pe.value_load(tile_expert[0:1, bass.ds(i, 1)], min_val=0, max_val=E - 1)
                pe.wait_ge(w2_ready, i + 1)
                if late(i, 2):
                    pe.wait_ge(y_ready, i - 1)
                for c in range(KH):
                    if c % 4 == 0:
                        pe.wait_ge(hlo_ready, 2 * i + c // 4 + 1)
                    chunk = CPL + c * D // CH
                    low = wsp[:, bass.ds(e * (CPE * 2 * CH) + chunk * 2 * CH + CH + c * D % CH, D)]
                    high = w2s[:, b, c * D:(c + 1) * D]
                    for hp, w in ((0, high), (1, high), (0, low)):
                        last = t_.matmul(ps_y[b], hT[:, b, hp, c * P:(c + 1) * P], w,
                                         start=(c == 0 and w is high and hp == 0), stop=(c == KH - 1 and w is low))
                last.then_inc(y_ps, 1)

            used = load_used(pe)
            turn_x(0, 0, 0, 1)

            def tile(i, b, r, turn, plan=None):
                e = pe.value_load(tile_expert[0:1, bass.ds(i, 1)], min_val=0, max_val=E - 1)
                if_used(pe, used, i + 1, lambda: turn_x(i + 1, 1 - b, (r + 1) % RING, turn + (1 if r == RING - 1 else 0)))
                if_used(pe, used, i, lambda: layer1(i, b, e))
                if late(i, 1):
                    if_used(pe, used, i - 1, lambda: layer2(i - 1, 1 - b))

            slot_tiles(pe, tile, plans=False)
            i = SLOT_TILES - 1
            if_used(pe, used, i, lambda: layer2(i, i % 2))


def kernel(x, cond_8, L0_cond_weight, L0_cond_mask, L0_cond_bias, L0_ffn_gate_w, L0_ffn_gate_b,
           L0_ffn_w1, L0_ffn_b1, L0_ffn_w2, L0_ffn_b2):
    import numpy as np
    import concourse.bacc as bacc
    from concourse.bass_utils import run_bass_kernel_spmd

    def c(a):
        return np.ascontiguousarray(a)

    def padded_gate(a):
        return np.tile(np.pad(a, ((0, 0), (0, EP - E))), (1, CG))

    x, y, cw, cm, cb, gw, gb, w1, b1, w2, b2 = map(np.asarray, (
        x, cond_8, L0_cond_weight, L0_cond_mask, L0_cond_bias, L0_ffn_gate_w, L0_ffn_gate_b,
        L0_ffn_w1, L0_ffn_b1, L0_ffn_w2, L0_ffn_b2))
    rows = x.reshape(TOK, D)
    w1_l = w1.transpose(0, 2, 1).reshape(E, KD, P, H).transpose(0, 2, 1, 3).reshape(E, P, D * H // P)
    w2_l = w2.transpose(0, 2, 1).reshape(E, KH, P, D).transpose(0, 2, 1, 3).reshape(E, P, D * H // P)
    arrays = {
        "x_t": c(rows.T.reshape(KD, P, TOK).transpose(1, 0, 2)),
        "x_rows": c(rows),
        "cond_y": c(y.reshape(B * G)),
        "cond_w": c(cw.reshape(4, 2, KD, P, D).transpose(0, 3, 1, 2, 4).reshape(4, P, 2, CW)),
        "cond_mask": c(cm.reshape(KD, P, D).transpose(1, 0, 2).reshape(P, CW)),
        "cond_bias": c(cb),
        "gate_t": padded_gate(gw.T).reshape(KD, P, CG * EP).transpose(1, 0, 2).copy(),
        "gate_b": padded_gate(gb[None, :]).reshape(P, 1),
        "w_all": c(np.concatenate([w1_l, w2_l], axis=2)),
        "b1": c(b1.reshape(E * KH, P)),
        "b2": c(b2),
    }
    nc = bacc.Bacc("TRN2", target_bir_lowering=False, num_devices=1)
    args = [nc.dram_tensor(n, a.shape, mybir.dt.from_np(a.dtype), kind="ExternalInput").ap() for n, a in arrays.items()]
    out = nc.dram_tensor("out", (TOK, D), F32, kind="ExternalOutput").ap()
    build(nc, *args, out)
    r = run_bass_kernel_spmd(nc, [arrays], core_ids=[0])
    return r.results[0]["out"].reshape(B, S, D)
```
